# Optimizing a Trainium2 kernel written in Bass

```python
import numpy as np
import jax
import jax.numpy as jnp

def _softmax(x, axis=-1):
    return jax.nn.softmax(x, axis=axis)

def _gelu(x):
    return jax.nn.gelu(x, approximate=True)

def _silu(x):
    return jax.nn.silu(x)

def _sigmoid(x):
    return jax.nn.sigmoid(x)

def _layernorm(x, axis=-1, eps=1e-05):
    m = jnp.mean(x, axis=axis, keepdims=True)
    v = jnp.var(x, axis=axis, keepdims=True)
    return (x - m) / jnp.sqrt(v + eps)

def _scatter_add(tgt, idx, src, axis=0):
    return tgt.at[idx].add(src)

def _segment_sum(src, seg, n):
    return jax.ops.segment_sum(src, seg, n)
kernel_name = 'mk_seq_preln_d1_jaxref_r8_6217fe'

def setup_inputs(seed: int=0):
    np.random.seed(seed)
    _w = jnp.asarray

    def _L0_attn_setup():
        import jax, jax.numpy as jnp
        import numpy as np
        D_MODEL = 128
        N_LAYERS = 2
        N_HEADS = 16
        HEAD_DIM = D_MODEL // N_HEADS
        D_FFN = 4 * D_MODEL
        B, L = (4, 128)

        def layer_norm(x, g, b, eps=1e-05):
            mu = jnp.mean(x, axis=-1, keepdims=True)
            var = jnp.var(x, axis=-1, keepdims=True)
            return (x - mu) * jax.lax.rsqrt(var + eps) * g + b

        def make_decay(length):
            gamma = 1.0 - 2.0 ** (-5.0 - jnp.arange(N_HEADS, dtype=jnp.float32))
            n = jnp.arange(length, dtype=jnp.float32)[:, None]
            m = jnp.arange(length, dtype=jnp.float32)[None, :]
            diff = n - m
            pow_ = gamma[:, None, None] ** diff[None]
            return jnp.where(diff[None] >= 0, pow_, 0.0)

        def _forward(x, proj_w, proj_b, reto_w, reto_b, ln1_g, ln1_b, ln2_g, ln2_b, ffn1_w, ffn1_b, ffn2_w, ffn2_b, lnf_g, lnf_b):
            Bx, Lx, _ = x.shape
            D = make_decay(Lx)
            for i in range(N_LAYERS):
                ln_x = layer_norm(x, ln1_g[i], ln1_b[i])
                p = ln_x @ proj_w[i] + proj_b[i]
                q, k, v, xo = jnp.split(p, 4, axis=-1)
                q = q.reshape(Bx, Lx, N_HEADS, HEAD_DIM).transpose(0, 2, 1, 3)
                k = k.reshape(Bx, Lx, N_HEADS, HEAD_DIM).transpose(0, 2, 1, 3)
                v = v.reshape(Bx, Lx, N_HEADS, HEAD_DIM).transpose(0, 2, 1, 3)
                scores = jnp.einsum('bhld,bhmd->bhlm', q, k) * D[None]
                ret = jnp.einsum('bhlm,bhmd->bhld', scores, v)
                ret = ret.transpose(0, 2, 1, 3).reshape(Bx, Lx, D_MODEL)
                ret = ret * jax.nn.silu(xo)
                ret = ret @ reto_w[i] + reto_b[i]
                x = x + ret
                h = layer_norm(x, ln2_g[i], ln2_b[i])
                h = jax.nn.gelu(h @ ffn1_w[i] + ffn1_b[i], approximate=False) @ ffn2_w[i] + ffn2_b[i]
                x = x + h
            return layer_norm(x, lnf_g, lnf_b)
        key = jax.random.key(seed)
        ks = jax.random.split(key, 16)
        s = 0.02
        inp = {'x': jax.random.normal(ks[0], (B, L, D_MODEL), jnp.float32), 'proj_w': jax.random.normal(ks[1], (N_LAYERS, D_MODEL, 4 * D_MODEL), jnp.float32) * s, 'proj_b': jnp.zeros((N_LAYERS, 4 * D_MODEL), jnp.float32), 'reto_w': jax.random.normal(ks[2], (N_LAYERS, D_MODEL, D_MODEL), jnp.float32) * s, 'reto_b': jnp.zeros((N_LAYERS, D_MODEL), jnp.float32), 'ln1_g': jnp.ones((N_LAYERS, D_MODEL), jnp.float32), 'ln1_b': jnp.zeros((N_LAYERS, D_MODEL), jnp.float32), 'ln2_g': jnp.ones((N_LAYERS, D_MODEL), jnp.float32), 'ln2_b': jnp.zeros((N_LAYERS, D_MODEL), jnp.float32), 'ffn1_w': jax.random.normal(ks[3], (N_LAYERS, D_MODEL, D_FFN), jnp.float32) * s, 'ffn1_b': jnp.zeros((N_LAYERS, D_FFN), jnp.float32), 'ffn2_w': jax.random.normal(ks[4], (N_LAYERS, D_FFN, D_MODEL), jnp.float32) * s, 'ffn2_b': jnp.zeros((N_LAYERS, D_MODEL), jnp.float32), 'lnf_g': jnp.ones((D_MODEL,), jnp.float32), 'lnf_b': jnp.zeros((D_MODEL,), jnp.float32)}
        return inp
    _L0_attn_in = _L0_attn_setup()

    def _L0_ffn_setup():
        import jax, jax.numpy as jnp
        import numpy as np
        MAX_VAL = 100.0
        key = jax.random.key(seed)
        k1, k2, k3 = jax.random.split(key, 3)
        B, S, D_IN, D_OUT = (4, 1024, 128, 128)
        x = jax.random.normal(k1, (B, S, D_IN), dtype=jnp.float32)
        weights = jax.random.normal(k2, (D_OUT, D_IN), dtype=jnp.float32)
        scale = jnp.ones((D_OUT,), dtype=jnp.float32)
        bias = jax.random.normal(k3, (D_OUT,), dtype=jnp.float32)
        return {'x': x, 'weights': weights, 'scale': scale, 'bias': bias}
    _L0_ffn_in = _L0_ffn_setup()
    _d = {'L0_attn_x': _L0_attn_in['x'], 'L0_attn_proj_w': _L0_attn_in['proj_w'], 'L0_attn_proj_b': _L0_attn_in['proj_b'], 'L0_attn_reto_w': _L0_attn_in['reto_w'], 'L0_attn_reto_b': _L0_attn_in['reto_b'], 'L0_attn_ln1_g': _L0_attn_in['ln1_g'], 'L0_attn_ln1_b': _L0_attn_in['ln1_b'], 'L0_attn_ln2_g': _L0_attn_in['ln2_g'], 'L0_attn_ln2_b': _L0_attn_in['ln2_b'], 'L0_attn_ffn1_w': _L0_attn_in['ffn1_w'], 'L0_attn_ffn1_b': _L0_attn_in['ffn1_b'], 'L0_attn_ffn2_w': _L0_attn_in['ffn2_w'], 'L0_attn_ffn2_b': _L0_attn_in['ffn2_b'], 'L0_attn_lnf_g': _L0_attn_in['lnf_g'], 'L0_attn_lnf_b': _L0_attn_in['lnf_b'], 'L0_ffn_weights': _L0_ffn_in['weights'], 'L0_ffn_scale': _L0_ffn_in['scale'], 'L0_ffn_bias': _L0_ffn_in['bias']}
    _x0 = _d['L0_attn_x']
    _d['L0_attn_x'] = jax.random.normal(jax.random.fold_in(jax.random.key(seed), 1), (8, 1024, 128), dtype=_x0.dtype)
    del _x0
    return _d

def reference(L0_attn_x, L0_attn_proj_w, L0_attn_proj_b, L0_attn_reto_w, L0_attn_reto_b, L0_attn_ln1_g, L0_attn_ln1_b, L0_attn_ln2_g, L0_attn_ln2_b, L0_attn_ffn1_w, L0_attn_ffn1_b, L0_attn_ffn2_w, L0_attn_ffn2_b, L0_attn_lnf_g, L0_attn_lnf_b, L0_ffn_weights, L0_ffn_scale, L0_ffn_bias):

    def _L0_attn_ref(x, proj_w, proj_b, reto_w, reto_b, ln1_g, ln1_b, ln2_g, ln2_b, ffn1_w, ffn1_b, ffn2_w, ffn2_b, lnf_g, lnf_b):
        import jax, jax.numpy as jnp
        import numpy as np
        D_MODEL = 128
        N_LAYERS = 2
        N_HEADS = 16
        HEAD_DIM = D_MODEL // N_HEADS
        D_FFN = 4 * D_MODEL
        B, L = (4, 128)

        def layer_norm(x, g, b, eps=1e-05):
            mu = jnp.mean(x, axis=-1, keepdims=True)
            var = jnp.var(x, axis=-1, keepdims=True)
            return (x - mu) * jax.lax.rsqrt(var + eps) * g + b

        def make_decay(length):
            gamma = 1.0 - 2.0 ** (-5.0 - jnp.arange(N_HEADS, dtype=jnp.float32))
            n = jnp.arange(length, dtype=jnp.float32)[:, None]
            m = jnp.arange(length, dtype=jnp.float32)[None, :]
            diff = n - m
            pow_ = gamma[:, None, None] ** diff[None]
            return jnp.where(diff[None] >= 0, pow_, 0.0)

        def _forward(x, proj_w, proj_b, reto_w, reto_b, ln1_g, ln1_b, ln2_g, ln2_b, ffn1_w, ffn1_b, ffn2_w, ffn2_b, lnf_g, lnf_b):
            Bx, Lx, _ = x.shape
            D = make_decay(Lx)
            for i in range(N_LAYERS):
                ln_x = layer_norm(x, ln1_g[i], ln1_b[i])
                p = ln_x @ proj_w[i] + proj_b[i]
                q, k, v, xo = jnp.split(p, 4, axis=-1)
                q = q.reshape(Bx, Lx, N_HEADS, HEAD_DIM).transpose(0, 2, 1, 3)
                k = k.reshape(Bx, Lx, N_HEADS, HEAD_DIM).transpose(0, 2, 1, 3)
                v = v.reshape(Bx, Lx, N_HEADS, HEAD_DIM).transpose(0, 2, 1, 3)
                scores = jnp.einsum('bhld,bhmd->bhlm', q, k) * D[None]
                ret = jnp.einsum('bhlm,bhmd->bhld', scores, v)
                ret = ret.transpose(0, 2, 1, 3).reshape(Bx, Lx, D_MODEL)
                ret = ret * jax.nn.silu(xo)
                ret = ret @ reto_w[i] + reto_b[i]
                x = x + ret
                h = layer_norm(x, ln2_g[i], ln2_b[i])
                h = jax.nn.gelu(h @ ffn1_w[i] + ffn1_b[i], approximate=False) @ ffn2_w[i] + ffn2_b[i]
                x = x + h
            return layer_norm(x, lnf_g, lnf_b)
        return _forward(x, proj_w, proj_b, reto_w, reto_b, ln1_g, ln1_b, ln2_g, ln2_b, ffn1_w, ffn1_b, ffn2_w, ffn2_b, lnf_g, lnf_b)

    def _L0_ffn_ref(x, weights, scale, bias):
        import jax, jax.numpy as jnp
        import numpy as np
        MAX_VAL = 100.0
        w = (weights >= 0.0).astype(x.dtype) * 2.0 - 1.0
        y = jnp.einsum('bsi,oi->bso', x, w)
        y = y * scale + bias
        y = jnp.clip(y, -MAX_VAL, MAX_VAL)
        return y
    x = L0_attn_x
    x = x + _L0_attn_ref(_layernorm(x, axis=-1), L0_attn_proj_w, L0_attn_proj_b, L0_attn_reto_w, L0_attn_reto_b, L0_attn_ln1_g, L0_attn_ln1_b, L0_attn_ln2_g, L0_attn_ln2_b, L0_attn_ffn1_w, L0_attn_ffn1_b, L0_attn_ffn2_w, L0_attn_ffn2_b, L0_attn_lnf_g, L0_attn_lnf_b)
    x = x + _L0_ffn_ref(_layernorm(x, axis=-1), L0_ffn_weights, L0_ffn_scale, L0_ffn_bias)
    return x

_drawn_inputs = setup_inputs


def setup_inputs(seed=0):
    import zlib

    import numpy as np

    out = dict(_drawn_inputs(seed))
    spreads = {'L0_attn_proj_b': (0.0, 0.1),
     'L0_attn_reto_b': (0.0, 0.1),
     'L0_attn_ln1_g': (1.0, 0.576),
     'L0_attn_ln1_b': (0.0, 0.336),
     'L0_attn_ln2_g': (1.0, 0.6),
     'L0_attn_ln2_b': (0.0, 0.8),
     'L0_attn_ffn1_b': (0.0, 0.479),
     'L0_attn_ffn2_b': (0.0, 0.1),
     'L0_attn_lnf_g': (1.0, 0.2),
     'L0_attn_lnf_b': (0.0, 0.1),
     'L0_ffn_scale': (1.0, 0.2)}
    factors = {}
    for name, (base, spread) in spreads.items():
        noise = np.random.default_rng([zlib.crc32(name.encode()), seed]).standard_normal(out[name].shape)
        drawn = base * np.exp(spread * noise) if base else spread * noise
        out[name] = jnp.asarray(drawn.astype(out[name].dtype))
    for name, factor in factors.items():
        out[name] = (out[name] * factor).astype(out[name].dtype)
    return out
```

```python
from contextlib import ExitStack

import numpy as np

import concourse.bass as bass
from concourse import mybir

P = 128
BATCH, LENGTH, WIDTH = 8, 1024, 128
HEADS, LAYERS, HIDDEN = 16, 2, 512
DH = WIDTH // HEADS
STREAMS = 2
TILES = BATCH // STREAMS
GROUP = TILES * P
STEPS = LENGTH // P
CHUNK = 32
CHUNKS = P // CHUNK
QUAD = 4
OUTS = 4
HC = HIDDEN // P
EPS = 1e-5
CLIP = 100.0
PHASES = 2 * LAYERS
DEPTH = [P - CHUNK * c for c in range(CHUNKS)]
S_AT = [QUAD * sum(DEPTH[:c]) for c in range(CHUNKS)]
S_WIDTH = QUAD * sum(DEPTH)

COL_G1, COL_B1, COL_G2, COL_B2 = 0, 2, 4, 6
COL_PB = 8
COL_F1B = COL_PB + LAYERS * OUTS
COLS = COL_F1B + LAYERS * HC
ROW_RB, ROW_F2B, ROW_LG, ROW_LB, ROW_SC, ROW_BI = 0, 2, 4, 5, 6, 7
ROWS = 8
C_DQ, C_DK, C_SM, C_ID, C_CM, C_JM = 0, P, 2 * P, 3 * P, 4 * P, 5 * P
CONSTS = 5 * P + QUAD

F32 = mybir.dt.float32
F32R = mybir.dt.float32r
ALU = mybir.AluOpType
ACT = mybir.ActivationFunctionType


class Turn:

    def __init__(self, i, c):
        self.i, self.c = i, c

    def after(self, n):
        return Turn(self.i, self.c + n)

    @property
    def stream(self):
        return self.c % STREAMS

    @property
    def layer(self):
        return (self.c // STREAMS) % LAYERS

    def count(self, per, k=0):
        return self.i * (PHASES * per) + (per * self.c + k)

    def past(self, n=1):
        return not isinstance(self.i, int) or PHASES * self.i + self.c >= n

    def past_groups(self, n=1):
        return not isinstance(self.i, int) or self.group(1) >= n

    @property
    def final(self):
        return isinstance(self.i, int) and PHASES * self.i + self.c == PHASES * STEPS - 1

    def group(self, per, k=0):
        return self.i * (STREAMS * per) + (per * (self.c // PHASES * STREAMS + self.stream) + k)

    def step(self, per, k=0):
        return self.i * per + (per * (self.c // PHASES) + k)


def retention_ffn(nc, x, columns, rows, consts, proj_w, reto_w, ffn1_w, ffn2_w, sign_w, out):
    x_v = x.rearrange("(s j) (t p) d -> s t p j d", s=STREAMS, p=P)
    out_v = out.rearrange("(s j) (t p) d -> s t p j d", s=STREAMS, p=P)

    with ExitStack() as ctx:
        def sb(name, shape, dt=F32):
            return ctx.enter_context(nc.sbuf_tensor(name, shape, dt))

        def bank(name):
            return ctx.enter_context(nc.psum_tensor(name, [P, GROUP], F32))

        def sem(name):
            return ctx.enter_context(nc.semaphore(name))

        col = sb("col", [P, COLS])
        row = sb("row", [P, ROWS, WIDTH])
        con = sb("con", [P, CONSTS])
        wp = sb("wp", [P, LAYERS, OUTS * P])
        wp_g = sb("wp_g", [P, LAYERS, OUTS * P])
        wp_h = sb("wp_h", [P, LAYERS, OUTS * P], F32R)
        wp_l = sb("wp_l", [P, LAYERS, OUTS * P], F32R)
        w1 = sb("w1", [P, LAYERS, HIDDEN])
        w1_g = sb("w1_g", [P, LAYERS, HIDDEN])
        w1_h = sb("w1_h", [P, LAYERS, HIDDEN], F32R)
        w1_l = sb("w1_l", [P, LAYERS, HIDDEN], F32R)
        w2 = sb("w2", [P, LAYERS, HC, WIDTH])
        wo_in = sb("wo_in", [P, LAYERS, WIDTH])
        wo = sb("wo", [P, LAYERS, WIDTH])
        ws_in = sb("ws_in", [P, WIDTH])
        ws_ge = sb("ws_ge", [P, WIDTH])
        ws = sb("ws", [P, WIDTH])
        pbias = sb("pbias", [P, LAYERS * OUTS])
        hbias = sb("hbias", [P, LAYERS])
        f1bias = sb("f1bias", [P, LAYERS * HC])
        xin = [sb(f"xin{s}", [P, TILES, WIDTH]) for s in range(STREAMS)]
        X = [sb(f"X{s}", [P, TILES, WIDTH]) for s in range(STREAMS)]
        XO = [sb(f"XO{s}", [P, TILES, WIDTH]) for s in range(STREAMS)]
        XRB = [sb(f"XRB{s}", [P, TILES, WIDTH]) for s in range(STREAMS)]
        OUT = [sb(f"OUT{s}", [P, TILES, WIDTH]) for s in range(STREAMS)]
        idle, held = sb("idle", [P, 1]), sb("held", [P, 1])
        st1, st2, st3, st4 = (sb(f"st{n}", [P, TILES, 6]) for n in range(1, 5))
        mv1, mv2, mv3, mv4 = (sb(f"mv{n}", [P, TILES, 2]) for n in range(1, 5))
        vv1, rs1 = sb("vv1", [P, 2, TILES]), sb("rs1", [P, 2, TILES])
        vv2, vv3, vv4, rs2, rs3, rs4 = (sb(n, [P, TILES]) for n in ("vv2", "vv3", "vv4", "rs2", "rs3", "rs4"))
        power = sb("power", [P, 2, TILES])
        Z1, Z2, Z4 = (sb(f"Z{n}", [P, TILES, WIDTH]) for n in (1, 2, 4))
        z1_h, z2_h, z1_l, z2_l = (sb(n, [P, GROUP], F32R) for n in ("z1_h", "z2_h", "z1_l", "z2_l"))
        z4_t = sb("z4_t", [P, GROUP])
        Y3, YG, U3, YS, YB, YC = (sb(n, [P, TILES, WIDTH]) for n in ("Y3", "YG", "U3", "YS", "YB", "YC"))
        q_in, k_in, v_in, xo_in, th = (sb(n, [P, TILES, P]) for n in ("q_in", "k_in", "v_in", "xo_in", "th"))
        qd = sb("qd", [P, TILES, P])
        kd = sb("kd", [P, TILES, P])
        qx = sb("qx", [P, QUAD, TILES, P])
        kx = sb("kx", [P, TILES * CHUNKS, QUAD, CHUNK])
        kt = sb("kt", [P, TILES, WIDTH])
        vt = sb("vt", [P, TILES, WIDTH])
        vx = sb("vx", [P, TILES, CHUNKS, QUAD, CHUNK])
        S = [sb(f"S{n}", [P, S_WIDTH]) for n in range(2)]
        gate = sb("gate", [P, TILES, P])
        gated = sb("gated", [P, TILES, P])
        state = sb("state", [P, LAYERS, STREAMS, TILES, WIDTH])
        state_sum = sb("state_sum", [P, TILES, WIDTH])
        hid = sb("hid", [P, HC, TILES, P])

        R = [bank(f"R{n}") for n in range(3)]
        RET = bank("RET")
        M = bank("M")
        F = [bank(f"F{n}") for n in range(2)]
        F2 = bank("F2")

        params = sem("params")
        x_in = [sem(f"x_in{s}") for s in range(STREAMS)]
        stored = [sem(f"stored{s}") for s in range(STREAMS)]
        zeroed = sem("zeroed")
        prep = sem("prep")
        prep_pe = sem("prep_pe")
        prep_act = sem("prep_act")
        rs1_ok, rs2_ok, rs3_ok, rs4_ok = (sem(f"rs{n}_ok") for n in range(1, 5))
        ln1, z1_ok, z1_t, z1_hok, z1_lok = (sem(n) for n in ("ln1", "z1_ok", "z1_t", "z1_hok", "z1_lok"))
        ln2, z2_ok, z2_t, z2_hok, z2_lok = (sem(n) for n in ("ln2", "z2_ok", "z2_t", "z2_hok", "z2_lok"))
        projected, proj_out = sem("projected"), sem("proj_out")
        kd_ok, qd_ok, kx_ok, qx_ok = (sem(n) for n in ("kd_ok", "qd_ok", "kx_ok", "qx_ok"))
        tm_t, tm_out, vx_ok = sem("tm_t"), sem("tm_out"), sem("vx_ok")
        scored, masked, ret_done = sem("scored"), sem("masked"), sem("ret_done")
        summed, sum_out, state_ok = sem("summed"), sem("sum_out"), sem("state_ok")
        gate_ok, gated_ok, reto_done, res1 = (sem(n) for n in ("gate_ok", "gated_ok", "reto_done", "res1"))
        xb1, xb2 = sem("xb1"), sem("xb2")
        ffn1_done, gelu_ok, ffn2_done, res2 = (sem(n) for n in ("ffn1_done", "gelu_ok", "ffn2_done", "res2"))
        ln3, y3_ok, yg_ok, u3_ok, ln4, z4_ok, z4_tt, z4_tok = (
            sem(n) for n in ("ln3", "y3_ok", "yg_ok", "u3_ok", "ln4", "z4_ok", "z4_tt", "z4_tok"))
        signed, ys_ok, yb_ok, yc_ok, out_ok, xrb_ok = (
            sem(n) for n in ("signed", "ys_ok", "yb_ok", "yc_ok", "out_ok", "xrb_ok"))

        ident = con[:, C_ID:C_ID + P]
        PARAMS_IN = 16 * 8
        PREP = 14
        IDENTITY = ACT.Identity

        def over_tiles(ap):
            return ap.unsqueeze(1).to_broadcast([P, TILES, ap.shape[-1]])

        def steps(play):
            def body(i, peeled):
                for c in range(PHASES):
                    play(Turn(i, c), True, True, c in (0, 3) and not (peeled and c == 0))
            play(Turn(0, -1), True, False, False)
            body(0, True)
            return body

        def run(eng, play):
            body = steps(play)
            with eng.Fori(1, STEPS - 1) as i:
                body(i, False)
            last = STEPS - 1
            for c in range(PHASES):
                play(Turn(last, c), c < PHASES - 1, True, c in (0, 3))
            play(Turn(last, PHASES), False, False, True)

        block = ctx.enter_context(nc.Block())

        @block.sync
        def _(sp):
            for s in range(STREAMS):
                sp.dma_start(xin[s][:, :, :], x_v[s, 0]).then_inc(x_in[s], 16)
            sp.dma_start(col[:, :], columns).then_inc(params, 16)
            sp.dma_start(row[:, :, :], rows.partition_broadcast(P)).then_inc(params, 16)
            sp.dma_start(con[:, :], consts).then_inc(params, 16)
            sp.dma_start(wp[:, :, :], proj_w.rearrange("l p n -> p l n")).then_inc(params, 16)
            sp.dma_start(w1[:, :, :], ffn1_w.rearrange("l p n -> p l n")).then_inc(params, 16)
            sp.dma_start(wo_in[:, :, :], reto_w.rearrange("l p n -> p l n")).then_inc(params, 16)
            sp.dma_start(w2[:, :, :, :], ffn2_w.rearrange("l (c p) n -> p l c n", p=P)).then_inc(params, 16)
            sp.dma_start(ws_in[:, :], sign_w).then_inc(params, 16)

            def loads(i):
                r = Turn(i, STREAMS - 1)
                sp.wait_ge(z1_ok, r.count(1, 1))
                sp.wait_ge(xrb_ok, r.group(1, 1))
                for s in range(STREAMS):
                    sp.dma_start(xin[s][:, :, :], x_v[s, 1:][i]).then_inc(x_in[s], 16)

            with sp.Fori(0, STEPS - 1) as i:
                loads(i)
                sp.wait_ge(out_ok, Turn(i, STREAMS - 1).group(1, 1))
                for s in reversed(range(STREAMS)):
                    sp.dma_start(out_v[s, i], OUT[s][:, :, :]).then_inc(stored[s], 16)
            for s in range(STREAMS):
                sp.wait_ge(out_ok, Turn(STEPS - 1, s).group(1, 1))
                sp.dma_start(out_v[s, STEPS - 1], OUT[s][:, :, :]).then_inc(stored[s], 16)
            for s in range(STREAMS):
                sp.wait_ge(stored[s], 16 * STEPS)

        @block.tensor
        def _(pe):
            def split_product(dst, w_h, w_l, z_h, z_l, low_ok, value):
                nc.tensor.matmul(dst, w_h, z_h, start=True, stop=False)
                nc.tensor.matmul(dst, w_l, z_h, start=False, stop=False)
                pe.wait_ge(low_ok, value)
                return nc.tensor.matmul(dst, w_h, z_l, start=False, stop=True)

            def transposes(dst, src):
                for t in range(TILES):
                    last = nc.tensor.transpose(dst[:, t * P:(t + 1) * P], src[:, t, :], ident)
                return last

            def z1_transposes(r):
                pe.wait_ge(z1_ok, r.count(1, 1))
                if r.past():
                    pe.wait_ge(sum_out, r.count(1, 0))
                transposes(M, Z1).then_inc(z1_t, 1)

            def play(s, has_r, has_f, has_o):
                r, f, o = s.after(1), s, s.after(-1)
                st, ly = r.stream, r.layer
                if has_r:
                    for n in range(OUTS):
                        if n == 0:
                            pe.wait_ge(z1_hok, r.count(1, 1))
                            if r.past():
                                pe.wait_ge(masked, r.count(4 * TILES, -3))
                        elif n == 1:
                            if r.past():
                                pe.wait_ge(masked, r.count(4 * TILES, -2))
                        elif n == 2:
                            if r.past():
                                pe.wait_ge(masked, r.count(4 * TILES, 0))
                        else:
                            pe.wait_ge(proj_out, r.count(OUTS, 1))
                        w = slice(n * P, (n + 1) * P)
                        split_product(R[n % 3][:, :], wp_h[:, ly, w], wp_l[:, ly, w], z1_h[:, :], z1_l[:, :],
                                      z1_lok, r.count(1, 1)).then_inc(projected, 1)
                if has_f:
                    pe.wait_ge(z2_ok, f.count(1, 1))
                    if f.past():
                        pe.wait_ge(res2, f.count(1, 0))
                    transposes(F2, Z2).then_inc(z2_t, 1)
                if has_r:
                    pe.wait_ge(kd_ok, r.count(1, 1))
                    pe.wait_ge(proj_out, r.count(OUTS, 2))
                    transposes(R[1], kd).then_inc(tm_t, 1)
                    pe.wait_ge(proj_out, r.count(OUTS, 3))
                    transposes(R[2], v_in).then_inc(tm_t, 1)
                if has_f:
                    fly = f.layer
                    for n in range(HC):
                        if n == 0:
                            pe.wait_ge(z2_hok, f.count(1, 1))
                        if n >= 2 or f.past():
                            pe.wait_ge(gelu_ok, f.count(HC, n - 1))
                        w = slice(n * P, (n + 1) * P)
                        split_product(F[n % 2][:, :], w1_h[:, fly, w], w1_l[:, fly, w], z2_h[:, :], z2_l[:, :],
                                      z2_lok, f.count(1, 1)).then_inc(ffn1_done, 1)
                if has_o:
                    pe.wait_ge(z4_ok, o.group(1, 1))
                    if has_r:
                        pe.wait_ge(z1_lok, r.count(1, 1))
                    transposes(M, Z4).then_inc(z4_tt, 1)

                def scores(t):
                    for c in range(CHUNKS):
                        n, w = min(c, 2), DEPTH[c]
                        if t == 0 and c == 0:
                            pe.wait_ge(qx_ok, r.count(1, 1))
                            pe.wait_ge(kx_ok, r.count(1, 1))
                            pe.wait_ge(proj_out, r.count(OUTS, 4))
                        elif t == 0 and c < 3:
                            pe.wait_ge(tm_out, r.count(2, c))
                        elif c < 3:
                            pe.wait_ge(masked, r.count(4 * TILES, 4 * t - (3, 2, 0)[c]))
                        at = 0 if c < 3 else QUAD * DEPTH[2]
                        dst = R[n][:, at:at + QUAD * w].rearrange("p (g n) -> p g n", g=QUAD)
                        mm = nc.tensor.matmul(
                            dst, kx[:, t * CHUNKS + c, :, :], qx[:, :, t, c * CHUNK:P],
                            start=True, stop=True, skip_group_check=True)
                        mm.then_inc(scored, 1)

                def retention(t):
                    cols = slice(t * P, (t + 1) * P)
                    if t == 0:
                        if r.past():
                            pe.wait_ge(res1, r.count(1, 0))
                        if r.past(PHASES):
                            pe.wait_ge(state_ok, r.count(1, 1 - PHASES))
                        pe.wait_ge(vx_ok, r.count(1, 1))
                    pe.wait_ge(masked, r.count(4 * TILES, 4 * t + 4))
                    nc.tensor.matmul(RET[:, cols], state[:, ly, st, t, :], qd[:, t, :],
                                     start=True, stop=False, skip_group_check=True)
                    for c in range(CHUNKS):
                        w = DEPTH[c]
                        for g in range(QUAD):
                            at = S_AT[c] + g * w
                            mm = nc.tensor.matmul(
                                RET[g * CHUNK:(g + 1) * CHUNK, t * P + c * CHUNK:(t + 1) * P],
                                vx[:, t, c, g, :], S[t % 2][:, at:at + w],
                                start=False, stop=(c == CHUNKS - 1), skip_group_check=True)
                    mm.then_inc(ret_done, 1)

                def sums(t):
                    if t == 0:
                        pe.wait_ge(tm_out, r.count(2, 2))
                        pe.wait_ge(z1_lok, r.count(1, 1))
                        if has_o:
                            pe.wait_ge(ys_ok, o.group(1, 1))
                    mm = nc.tensor.matmul(M[:, t * P:(t + 1) * P], kt[:, t, :], vt[:, t, :],
                                          start=True, stop=True, skip_group_check=True)
                    if t == TILES - 1:
                        mm.then_inc(summed, 1)

                def last_product():
                    pe.wait_ge(z4_tok, o.group(1, 1))
                    for t in range(TILES):
                        mm = nc.tensor.matmul(M[:, t * P:(t + 1) * P], z4_t[:, t * P:(t + 1) * P], ws[:, :],
                                              start=True, stop=True, skip_group_check=True)
                    mm.then_inc(signed, 1)

                def ffn2(t):
                    if t == 0:
                        pe.wait_ge(gelu_ok, f.count(HC, HC))
                        pe.wait_ge(z2_lok, f.count(1, 1))
                    for c in range(HC):
                        mm = nc.tensor.matmul(F2[:, t * P:(t + 1) * P], hid[:, c, t, :], w2[:, f.layer, c, :],
                                              start=(c == 0), stop=(c == HC - 1), skip_group_check=True)
                    if t == TILES - 1:
                        mm.then_inc(ffn2_done, 1)

                if has_r:
                    scores(0)
                if has_o:
                    last_product()
                if has_f:
                    ffn2(0)
                    ffn2(1)
                if has_r:
                    scores(1)
                    retention(0)
                if has_f:
                    ffn2(2)
                    ffn2(3)
                if has_r:
                    scores(2)
                    retention(1)
                    sums(0)
                    sums(1)
                    scores(3)
                    retention(2)
                    sums(2)
                    sums(3)
                    retention(3)
                    if not r.final:
                        z1_transposes(r.after(1))
                    pe.wait_ge(gated_ok, r.count(1, 1))
                    for t in range(TILES):
                        mm = nc.tensor.matmul(RET[:, t * P:(t + 1) * P], gated[:, t, :], wo[:, ly, :],
                                              start=True, stop=True, skip_group_check=True)
                    mm.then_inc(reto_done, 1)

            pe.wait_ge(params, PARAMS_IN)
            for n in range(LAYERS * OUTS):
                nc.tensor.matmul(F[0][:, n:n + 1], wp[:, n // OUTS, n % OUTS * P:(n % OUTS + 1) * P],
                                 col[:, COL_B1 + n // OUTS:COL_B1 + n // OUTS + 1],
                                 start=True, stop=True, skip_group_check=True)
            for n in range(LAYERS * HC):
                mm = nc.tensor.matmul(F[0][:, 16 + n:17 + n], w1[:, n // HC, n % HC * P:(n % HC + 1) * P],
                                      col[:, COL_B2 + n // HC:COL_B2 + n // HC + 1],
                                      start=True, stop=True, skip_group_check=True)
            mm.then_inc(prep_pe, 1)
            z1_transposes(Turn(0, 0))
            pe.wait_ge(prep, PREP)
            run(pe, play)

        @block.scalar
        def _(act):
            def high_part(dst, src):
                return nc.scalar.activation(dst, src, ACT.Copy)

            def z1_high(r):
                act.wait_ge(z1_t, r.count(1, 1))
                if r.past():
                    act.wait_ge(projected, r.count(OUTS, 0))
                high_part(z1_h[:, :], M[:, :]).then_inc(z1_hok, 1)

            def play(s, has_r, has_f, has_o):
                r, f, o = s.after(1), s, s.after(-1)
                ly = r.layer
                if has_r:
                    for n, dst in enumerate((q_in, k_in, v_in, xo_in)):
                        act.wait_ge(projected, r.count(OUTS, n + 1))
                        if n == 0:
                            if r.past():
                                act.wait_ge(qd_ok, r.count(1, 0))
                        elif n == 1:
                            if r.past():
                                act.wait_ge(kd_ok, r.count(1, 0))
                        elif n == 2:
                            if r.past():
                                act.wait_ge(tm_t, r.count(2, 0))
                        else:
                            if r.past():
                                act.wait_ge(gate_ok, r.count(1, 0))
                        bias = pbias[:, ly * OUTS + n:ly * OUTS + n + 1]
                        src = R[n % 3][:, :].rearrange("p (t n) -> p t n", t=TILES)
                        ins = nc.scalar.activation(dst[:, :, :], src, IDENTITY, bias=bias)
                        if n == 3:
                            ins = nc.scalar.activation(th[:, :, :], src, ACT.Tanh, scale=0.5, bias=hbias[:, ly:ly + 1])
                        ins.then_inc(proj_out, 1)
                if has_f:
                    act.wait_ge(z2_t, f.count(1, 1))
                    if f.past():
                        act.wait_ge(ffn1_done, f.count(HC, 0))
                    high_part(z2_h[:, :], F2[:, :]).then_inc(z2_hok, 1)
                if has_r:
                    act.wait_ge(tm_t, r.count(2, 1))
                    if r.past():
                        act.wait_ge(summed, r.count(1, 0))
                    nc.scalar.activation(kt[:, :, :], R[1][:, :].rearrange("p (t n) -> p t n", t=TILES),
                                         ACT.Copy).then_inc(tm_out, 1)
                    act.wait_ge(tm_t, r.count(2, 2))
                    nc.scalar.activation(vt[:, :, :], R[2][:, :].rearrange("p (t n) -> p t n", t=TILES),
                                         ACT.Copy).then_inc(tm_out, 1)
                    act.wait_ge(qd_ok, r.count(1, 1))
                    for g in range(QUAD):
                        rows_g = slice(g * CHUNK, (g + 1) * CHUNK)
                        ins = nc.scalar.copy(qx[rows_g, g, :, :], qd[rows_g, :, :])
                    ins.then_inc(qx_ok, 1)
                    act.wait_ge(tm_out, r.count(2, 2))
                    if r.past():
                        act.wait_ge(ret_done, r.count(TILES, 0))
                    for c in range(CHUNKS):
                        v = vt[c * CHUNK:(c + 1) * CHUNK, :, :].rearrange("p t (g j e) -> p t g j e", g=QUAD, j=QUAD)
                        for j in range(QUAD):
                            ins = nc.scalar.copy(
                                vx[j * CHUNK:(j + 1) * CHUNK, :, c, :, j * DH:(j + 1) * DH], v[:, :, :, j, :])
                    ins.then_inc(vx_ok, 1)
                if has_f:
                    fly = f.layer
                    for n in range(HC):
                        act.wait_ge(ffn1_done, f.count(HC, n + 1))
                        if n == 0:
                            if f.past():
                                act.wait_ge(ffn2_done, f.count(1, 0))
                        nc.scalar.activation(hid[:, n, :, :], F[n % 2][:, :].rearrange("p (t n) -> p t n", t=TILES),
                                             ACT.Gelu, bias=f1bias[:, fly * HC + n:fly * HC + n + 1]
                                             ).then_inc(gelu_ok, 1)
                if has_o:
                    act.wait_ge(z4_tt, o.group(1, 1))
                    if o.past_groups():
                        act.wait_ge(signed, o.group(1, 0))
                    nc.scalar.activation(z4_t[:, :], M[:, :], ACT.Copy).then_inc(z4_tok, 1)
                if has_r and not r.final:
                    z1_high(r.after(1))

            z1_high(Turn(0, 0))
            act.wait_ge(prep, PREP)
            act.wait_ge(zeroed, 1)
            run(act, play)

        @block.vector
        def _(dve):
            def statistics(src, st, mv, chain, value):
                for t in range(TILES):
                    ins = nc.vector.bn_stats(st[:, t, :], src[:, t, :])
                ins.then_inc(chain, 1)
                dve.wait_ge(chain, value(1))
                nc.vector.memset(idle[:, :], 0.0)
                for t in range(TILES):
                    ins = nc.vector.bn_aggr(mv[:, t, :], st[:, t, :])
                ins.then_inc(chain, 1)
                dve.wait_ge(chain, value(2))

            def normalise(dst, src, mv, rs):
                for t in range(TILES):
                    ins = nc.vector.tensor_scalar(dst[:, t, :], src[:, t, :], mv[:, t, 0:1], rs[:, t:t + 1],
                                                  ALU.subtract, ALU.mult)
                return ins

            def shifted(dst, mv):
                return nc.vector.tensor_scalar(dst, mv[:, :, 1], EPS, None, ALU.add)

            def first_norm(r):
                st, ly = r.stream, r.layer
                src = X[st] if ly else xin[st]
                if ly == 0:
                    dve.wait_ge(x_in[st], r.step(16, 16))
                else:
                    dve.wait_ge(res2, r.count(1, -1))
                statistics(src, st1, mv1, ln1, lambda k: r.count(3, k))
                if ly == 0:
                    shifted(vv1[:, 1, :], mv1)
                    nc.vector.tensor_scalar(vv1[:, 0, :], mv1[:, :, 1], 1.0 + EPS, EPS * EPS,
                                            ALU.mult, ALU.add).then_inc(ln1, 1)
                    dve.wait_ge(rs1_ok, r.count(1, 1))
                    normalise(X[st], src, mv1, rs1[:, 1, :])
                else:
                    shifted(vv1[:, 0, :], mv1).then_inc(ln1, 1)
                    dve.wait_ge(rs1_ok, r.count(1, 1))
                if r.past():
                    dve.wait_ge(z1_t, r.count(1, 0))
                normalise(Z1, src, mv1, rs1[:, 0, :]).then_inc(z1_ok, 1)

            def low_part(r, dst, src, high, sem_h, sem_l):
                dve.wait_ge(sem_h, r.count(1, 1))
                nc.vector.tensor_tensor(dst[:, :], src[:, :], high[:, :].bitcast(F32), ALU.subtract).then_inc(sem_l, 1)

            def play(s, has_r, has_f, has_o):
                r, f, o = s.after(1), s, s.after(-1)
                st, ly, fst, ost = r.stream, r.layer, f.stream, o.stream
                if has_f:
                    dve.wait_ge(reto_done, f.count(1, 1))
                    dve.wait_ge(xb1, f.count(1, 1))
                    nc.vector.tensor_tensor(X[fst][:, :, :], RET[:, :].rearrange("p (t n) -> p t n", t=TILES),
                                            X[fst][:, :, :], ALU.add).then_inc(res1, 1)
                    dve.wait_ge(res1, f.count(1, 1))
                    statistics(X[fst], st2, mv2, ln2, lambda k: f.count(3, k))
                    shifted(vv2[:, :], mv2).then_inc(ln2, 1)
                    dve.wait_ge(rs2_ok, f.count(1, 1))
                    if f.past():
                        dve.wait_ge(z2_t, f.count(1, 0))
                    normalise(Z2, X[fst], mv2, rs2).then_inc(z2_ok, 1)
                if has_o:
                    dve.wait_ge(res2, o.count(1, 1))
                    statistics(XO[ost], st3, mv3, ln3, lambda k: o.group(3, k))
                    shifted(vv3[:, :], mv3).then_inc(ln3, 1)
                    dve.wait_ge(rs3_ok, o.group(1, 1))
                    if o.past_groups():
                        dve.wait_ge(yg_ok, o.group(1, 0))
                    normalise(Y3, XO[ost], mv3, rs3).then_inc(y3_ok, 1)
                if has_r:
                    dve.wait_ge(proj_out, r.count(OUTS, 2))
                    if r.past():
                        dve.wait_ge(tm_t, r.count(2, -1))
                    nc.vector.tensor_tensor(kd[:, :, :], k_in[:, :, :], over_tiles(con[:, C_DK:C_DK + P]),
                                            ALU.mult).then_inc(kd_ok, 1)
                    if r.past():
                        dve.wait_ge(ret_done, r.count(TILES, 0))
                    nc.vector.tensor_tensor(qd[:, :, :], q_in[:, :, :], over_tiles(con[:, C_DQ:C_DQ + P]),
                                            ALU.mult).then_inc(qd_ok, 1)
                if has_f:
                    low_part(f, z2_l, F2, z2_h, z2_hok, z2_lok)
                if has_r:
                    dve.wait_ge(kd_ok, r.count(1, 1))
                    kd_chunks = kd[:, :, :].rearrange("p t (c n) -> p (t c) n", c=CHUNKS)
                    for j in range(QUAD):
                        ins = nc.vector.tensor_scalar(kx[:, :, j, :], kd_chunks, con[:, C_JM + j:C_JM + j + 1], None,
                                                      ALU.mult)
                    ins.then_inc(kx_ok, 1)
                if has_o:
                    dve.wait_ge(u3_ok, o.group(1, 1))
                    statistics(U3, st4, mv4, ln4, lambda k: o.group(3, k))
                    shifted(vv4[:, :], mv4).then_inc(ln4, 1)
                    dve.wait_ge(rs4_ok, o.group(1, 1))
                    if o.past_groups():
                        dve.wait_ge(z4_tt, o.group(1, 0))
                    normalise(Z4, U3, mv4, rs4).then_inc(z4_ok, 1)
                if has_r:
                    dve.wait_ge(proj_out, r.count(OUTS, 4))
                    if r.past():
                        dve.wait_ge(gated_ok, r.count(1, 0))
                    nc.vector.scalar_tensor_tensor(out=gate[:, :, :], in0=th[:, :, :], scalar=1.0, in1=xo_in[:, :, :],
                                                   op0=ALU.add, op1=ALU.mult).then_inc(gate_ok, 1)

                def mask(t):
                    for c in range(CHUNKS):
                        n, w = min(c, 2), DEPTH[c]
                        dve.wait_ge(scored, r.count(4 * TILES, 4 * t + (1, 2, 4, 4)[c]))
                        if c == 0:
                            if t >= 2 or r.past():
                                dve.wait_ge(ret_done, r.count(TILES, t - 1))
                        at = 0 if c < 3 else QUAD * DEPTH[2]
                        nc.vector.tensor_tensor(
                            S[t % 2][:, S_AT[c]:S_AT[c] + QUAD * w].rearrange("p (g n) -> p g n", g=QUAD),
                            R[n][:, at:at + QUAD * w].rearrange("p (g n) -> p g n", g=QUAD),
                            con[:, C_CM:C_CM + w].unsqueeze(1).to_broadcast([P, QUAD, w]),
                            ALU.mult).then_inc(masked, 1)

                if has_r:
                    mask(0)
                if has_o:
                    dve.wait_ge(signed, o.group(1, 1))
                    if o.past_groups():
                        dve.wait_ge(yb_ok, o.group(1, 0))
                    nc.vector.tensor_tensor(YS[:, :, :], M[:, :].rearrange("p (t n) -> p t n", t=TILES),
                                            over_tiles(row[:, ROW_SC, :]), ALU.mult).then_inc(ys_ok, 1)
                if has_r:
                    mask(1)
                if has_f:
                    dve.wait_ge(ffn2_done, f.count(1, 1))
                    dve.wait_ge(xb2, f.count(1, 1))
                    dst = XO if f.layer else X
                    nc.vector.tensor_tensor(dst[fst][:, :, :], F2[:, :].rearrange("p (t n) -> p t n", t=TILES),
                                            X[fst][:, :, :], ALU.add).then_inc(res2, 1)
                if has_r:
                    mask(2)
                    if not r.final:
                        first_norm(r.after(1))
                    mask(3)
                    dve.wait_ge(summed, r.count(1, 1))
                    if r.past():
                        dve.wait_ge(state_ok, r.count(1, 0))
                    nc.vector.tensor_tensor(state_sum[:, :, :], M[:, :].rearrange("p (t n) -> p t n", t=TILES),
                                            state[:, ly, st, :, :], ALU.add).then_inc(sum_out, 1)
                    dve.wait_ge(ret_done, r.count(TILES, TILES))
                    dve.wait_ge(gate_ok, r.count(1, 1))
                    if r.past():
                        dve.wait_ge(reto_done, r.count(1, 0))
                    nc.vector.tensor_tensor(gated[:, :, :], RET[:, :].rearrange("p (t n) -> p t n", t=TILES),
                                            gate[:, :, :], ALU.mult).then_inc(gated_ok, 1)
                    if not r.final:
                        dve.wait_ge(projected, r.count(OUTS, OUTS))
                        low_part(r.after(1), z1_l, M, z1_h, z1_hok, z1_lok)

            first_norm(Turn(0, 0))
            dve.wait_ge(params, PARAMS_IN)
            for w, g, w_g in ((wp, COL_G1, wp_g), (w1, COL_G2, w1_g)):
                for n in range(LAYERS):
                    nc.vector.tensor_scalar(w_g[:, n, :], w[:, n, :], col[:, g + n:g + n + 1], None,
                                            ALU.mult).then_inc(prep, 1)
            dve.wait_ge(prep, 4)
            nc.vector.tensor_copy(wp_h[:, :, :], wp_g[:, :, :]).then_inc(prep, 1)
            nc.vector.tensor_copy(w1_h[:, :, :], w1_g[:, :, :]).then_inc(prep, 1)
            dve.wait_ge(prep, 6)
            nc.vector.tensor_tensor(wp_l[:, :, :], wp_g[:, :, :], wp_h[:, :, :].bitcast(F32), ALU.subtract).then_inc(prep, 1)
            nc.vector.tensor_tensor(w1_l[:, :, :], w1_g[:, :, :], w1_h[:, :, :].bitcast(F32), ALU.subtract).then_inc(prep, 1)
            nc.vector.tensor_scalar(wo[:, :, :], wo_in[:, :, :], 0.5, None, ALU.mult).then_inc(prep, 1)
            nc.vector.tensor_scalar(ws_ge[:, :], ws_in[:, :], 0.0, 2.0, ALU.is_ge, ALU.mult).then_inc(prep, 1)
            dve.wait_ge(prep, 10)
            nc.vector.tensor_scalar(ws[:, :], ws_ge[:, :], -1.0, None, ALU.add).then_inc(prep, 1)
            dve.wait_ge(prep_pe, 1)
            nc.vector.tensor_tensor(pbias[:, :], F[0][:, 0:LAYERS * OUTS], col[:, COL_PB:COL_PB + LAYERS * OUTS],
                                    ALU.add).then_inc(prep, 1)
            nc.vector.tensor_tensor(f1bias[:, :], F[0][:, 16:16 + LAYERS * HC], col[:, COL_F1B:COL_F1B + LAYERS * HC],
                                    ALU.add).then_inc(prep, 1)
            dve.wait_ge(prep, 13)
            nc.vector.tensor_scalar(hbias[:, :], pbias[:, :].rearrange("p (l o) -> p l o", o=OUTS)[:, :, OUTS - 1],
                                    0.5, None, ALU.mult).then_inc(prep, 1)
            low_part(Turn(0, 0), z1_l, M, z1_h, z1_hok, z1_lok)
            dve.wait_ge(zeroed, 1)
            run(dve, play)

        @block.gpsimd
        def _(pool):
            def add_row(dst, a, n, op=ALU.add):
                return nc.gpsimd.tensor_tensor(dst[:, :, :], a[:, :, :], over_tiles(row[:, n, :]), op)

            def inverse_root(dst, src, ready, value, done):
                pool.wait_ge(ready, value)
                nc.gpsimd.tensor_tensor(dst, src, power[:, 0:dst.shape[1], :] if len(dst.shape) == 3 else power[:, 0, :],
                                        ALU.pow).then_inc(done, 1)

            def carry_wait():
                nc.gpsimd.tensor_tensor(held[:, :], power[:, 0, 0:1], power[:, 0, 0:1], ALU.mult)

            def input_copy(r):
                st = r.stream
                pool.wait_ge(x_in[st], r.step(16, 16))
                if r.past_groups(STREAMS):
                    pool.wait_ge(u3_ok, r.group(1, -1))
                add_row(XRB[st], xin[st], ROW_LB).then_inc(xrb_ok, 1)

            def after_first_norm(r):
                n = 1 if r.layer else 2
                inverse_root(rs1[:, 0:n, :], vv1[:, 0:n, :], ln1, r.count(3, 3), rs1_ok)
                pool.wait_ge(z1_ok, r.count(1, 1))
                add_row(X[r.stream], X[r.stream], ROW_RB + r.layer).then_inc(xb1, 1)

            def play(s, has_r, has_f, has_o):
                r, f, o = s.after(1), s, s.after(-1)
                st, ly, ost = r.stream, r.layer, o.stream
                if has_f:
                    inverse_root(rs2[:, :], vv2[:, :], ln2, f.count(3, 3), rs2_ok)
                    pool.wait_ge(z2_ok, f.count(1, 1))
                    add_row(X[f.stream], X[f.stream], ROW_F2B + f.layer).then_inc(xb2, 1)
                if has_o:
                    inverse_root(rs3[:, :], vv3[:, :], ln3, o.group(3, 3), rs3_ok)
                    pool.wait_ge(y3_ok, o.group(1, 1))
                    add_row(YG, Y3, ROW_LG, ALU.mult).then_inc(yg_ok, 1)
                    pool.wait_ge(yg_ok, o.group(1, 1))
                    pool.wait_ge(xrb_ok, o.group(1, 1))
                    nc.gpsimd.tensor_tensor(U3[:, :, :], YG[:, :, :], XRB[ost][:, :, :], ALU.add).then_inc(u3_ok, 1)
                    if not (isinstance(s.i, int) and s.i == STEPS - 1 and s.c > 0):
                        input_copy(o.after(2))
                if has_o:
                    inverse_root(rs4[:, :], vv4[:, :], ln4, o.group(3, 3), rs4_ok)
                if has_o:
                    pool.wait_ge(ys_ok, o.group(1, 1))
                    add_row(YB, YS, ROW_BI).then_inc(yb_ok, 1)
                    pool.wait_ge(yb_ok, o.group(1, 1))
                    carry_wait()
                    nc.gpsimd.tensor_scalar(YC[:, :, :], YB[:, :, :], CLIP, -CLIP, ALU.min, ALU.max).then_inc(yc_ok, 1)
                    pool.wait_ge(yc_ok, o.group(1, 1))
                    if o.past_groups(STREAMS):
                        pool.wait_ge(stored[ost], o.step(16, 0))
                    nc.gpsimd.tensor_tensor(OUT[ost][:, :, :], YC[:, :, :], U3[:, :, :], ALU.add).then_inc(out_ok, 1)
                if has_r:
                    if not r.final:
                        after_first_norm(r.after(1))
                    pool.wait_ge(sum_out, r.count(1, 1))
                    pool.wait_ge(ret_done, r.count(TILES, TILES))
                    nc.gpsimd.tensor_tensor(state[:, ly, st, :, :], state_sum[:, :, :],
                                            over_tiles(con[:, C_SM:C_SM + P]), ALU.mult).then_inc(state_ok, 1)

            nc.gpsimd.memset(power[:, :, :], -0.5)
            nc.gpsimd.memset(state[:, :, :, :, :], 0.0)
            nc.gpsimd.memset(qx[:, :, :, :], 0.0)
            nc.gpsimd.memset(vx[:, :, :, :, :], 0.0).then_inc(zeroed, 1)
            pool.wait_ge(zeroed, 1)
            pool.wait_ge(params, PARAMS_IN)
            for st in range(STREAMS):
                input_copy(Turn(0, st))
            after_first_norm(Turn(0, 0))
            run(pool, play)


def constants():
    head = np.arange(P) // DH
    gamma = 1.0 - 2.0 ** (-5.0 - head.astype(np.float64))
    n = np.arange(P)
    con = np.zeros((P, CONSTS), np.float64)
    con[:, C_DQ:C_DQ + P] = gamma[:, None] ** n[None, :]
    con[:, C_DK:C_DK + P] = gamma[:, None] ** -n[None, :].astype(np.float64)
    con[:, C_SM:C_SM + P] = (head[:, None] == head[None, :]) * gamma[:, None] ** P
    con[:, C_ID:C_ID + P] = np.eye(P)
    con[:, C_CM:C_CM + P] = (n[:, None] % CHUNK) <= n[None, :]
    con[:, C_JM:C_JM + QUAD] = (head[:, None] % QUAD) == np.arange(QUAD)[None, :]
    return con.astype(np.float32)


def kernel(**inputs):
    import concourse.bacc as bacc
    from concourse.bass_utils import run_bass_kernel_spmd

    a = {n: np.ascontiguousarray(v) for n, v in inputs.items()}

    def by_partition(v):
        return v.reshape(-1, P).T

    columns = np.concatenate([by_partition(a["L0_attn_" + n]) for n in (
        "ln1_g", "ln1_b", "ln2_g", "ln2_b", "proj_b", "ffn1_b")], axis=1)
    rows = np.concatenate([a[n].reshape(-1, WIDTH) for n in (
        "L0_attn_reto_b", "L0_attn_ffn2_b", "L0_attn_lnf_g", "L0_attn_lnf_b", "L0_ffn_scale", "L0_ffn_bias")], axis=0)
    arrays = {
        "x": a["L0_attn_x"], "columns": columns, "rows": rows, "consts": constants(),
        "proj_w": a["L0_attn_proj_w"], "reto_w": a["L0_attn_reto_w"], "ffn1_w": a["L0_attn_ffn1_w"],
        "ffn2_w": a["L0_attn_ffn2_w"], "sign_w": a["L0_ffn_weights"].T,
    }
    arrays = {n: np.ascontiguousarray(v) for n, v in arrays.items()}
    nc = bacc.Bacc("TRN2", target_bir_lowering=False, num_devices=1)
    args = [nc.dram_tensor(n + "_dram", v.shape, mybir.dt.from_np(v.dtype), kind="ExternalInput").ap()
            for n, v in arrays.items()]
    out = nc.dram_tensor("out_dram", arrays["x"].shape, F32, kind="ExternalOutput").ap()
    retention_ffn(nc, *args, out)
    r = run_bass_kernel_spmd(nc, [{n + "_dram": v for n, v in arrays.items()}], core_ids=[0])
    return r.results[0]["out_dram"]
```

```python
from contextlib import ExitStack

import numpy as np

import concourse.bass as bass
from concourse import mybir

P = 128
BATCH, LENGTH, WIDTH = 8, 1024, 128
HEADS, LAYERS, HIDDEN = 16, 2, 512
DH = WIDTH // HEADS
STREAMS = 2
TILES = BATCH // STREAMS
GROUP = TILES * P
STEPS = LENGTH // P
CHUNK = 32
CHUNKS = P // CHUNK
QUAD = 4
OUTS = 4
HC = HIDDEN // P
EPS = 1e-5
CLIP = 100.0
PHASES = 2 * LAYERS
HALVES = 2
HALF = P // HALVES
DEPTH = [HALF - c % (CHUNKS // HALVES) * CHUNK for c in range(CHUNKS)]
S_AT = [QUAD * sum(DEPTH[:c]) for c in range(CHUNKS)]
S_HALF = QUAD * sum(DEPTH) // HALVES

COL_G1, COL_B1, COL_G2, COL_B2 = 0, 2, 4, 6
COL_PB = 8
COL_F1B = COL_PB + LAYERS * OUTS
COLS = COL_F1B + LAYERS * HC
ROW_RB, ROW_F2B, ROW_LG, ROW_LB, ROW_SC, ROW_BI = 0, 2, 4, 5, 6, 7
ROWS = 8
C_DQ, C_DK, C_SM, C_BM, C_ID, C_CM = 0, P, 2 * P, 3 * P, 4 * P, 5 * P
C_JM = C_CM + S_HALF
CONSTS = C_JM + QUAD

F32 = mybir.dt.float32
F32R = mybir.dt.float32r
ALU = mybir.AluOpType
ACT = mybir.ActivationFunctionType


class Turn:

    def __init__(self, i, c):
        self.i, self.c = i, c

    def after(self, n):
        return Turn(self.i, self.c + n)

    @property
    def stream(self):
        return self.c % STREAMS

    @property
    def layer(self):
        return (self.c // STREAMS) % LAYERS

    def count(self, per, k=0):
        return self.i * (PHASES * per) + (per * self.c + k)

    def past(self, n=1):
        return not isinstance(self.i, int) or PHASES * self.i + self.c >= n

    def past_groups(self, n=1):
        return not isinstance(self.i, int) or self.group(1) >= n

    @property
    def final(self):
        return isinstance(self.i, int) and PHASES * self.i + self.c == PHASES * STEPS - 1

    def group(self, per, k=0):
        return self.i * (STREAMS * per) + (per * (self.c // PHASES * STREAMS + self.stream) + k)

    def step(self, per, k=0):
        return self.i * per + (per * (self.c // PHASES) + k)


def retention_ffn(nc, x, columns, rows, consts, proj_w, reto_w, ffn1_w, ffn2_w, sign_w, out):
    x_v = x.rearrange("(s j) (t p) d -> s t p j d", s=STREAMS, p=P)
    out_v = out.rearrange("(s j) (t p) d -> s t p j d", s=STREAMS, p=P)

    with ExitStack() as ctx:
        def sb(name, shape, dt=F32):
            return ctx.enter_context(nc.sbuf_tensor(name, shape, dt))

        def bank(name):
            return ctx.enter_context(nc.psum_tensor(name, [P, GROUP], F32))

        def sem(name):
            return ctx.enter_context(nc.semaphore(name))

        col = sb("col", [P, COLS])
        row = sb("row", [P, ROWS, WIDTH])
        con = sb("con", [P, CONSTS])
        wp = sb("wp", [P, LAYERS, OUTS * P])
        wp_g = sb("wp_g", [P, LAYERS, OUTS * P])
        wp_h = sb("wp_h", [P, LAYERS, OUTS * P], F32R)
        wp_l = sb("wp_l", [P, LAYERS, OUTS * P], F32R)
        w1 = sb("w1", [P, LAYERS, HIDDEN])
        w1_g = sb("w1_g", [P, LAYERS, HIDDEN])
        w1_h = sb("w1_h", [P, LAYERS, HIDDEN], F32R)
        w1_l = sb("w1_l", [P, LAYERS, HIDDEN], F32R)
        w2 = sb("w2", [P, LAYERS, HC, WIDTH])
        wo_in = sb("wo_in", [P, LAYERS, WIDTH])
        wo = sb("wo", [P, LAYERS, WIDTH])
        ws_in = sb("ws_in", [P, WIDTH])
        ws_ge = sb("ws_ge", [P, WIDTH])
        ws = sb("ws", [P, WIDTH])
        pbias = sb("pbias", [P, LAYERS * OUTS])
        hbias = sb("hbias", [P, LAYERS])
        f1bias = sb("f1bias", [P, LAYERS * HC])
        xin = [sb(f"xin{s}", [P, TILES, WIDTH]) for s in range(STREAMS)]
        X = [sb(f"X{s}", [P, TILES, WIDTH]) for s in range(STREAMS)]
        XO = [sb(f"XO{s}", [P, TILES, WIDTH]) for s in range(STREAMS)]
        XRB = [sb(f"XRB{s}", [P, TILES, WIDTH]) for s in range(STREAMS)]
        OUT = [sb(f"OUT{s}", [P, TILES, WIDTH]) for s in range(STREAMS)]
        idle, held = sb("idle", [P, 1]), sb("held", [P, 1])
        st1, st2, st3, st4 = (sb(f"st{n}", [P, TILES, 6]) for n in range(1, 5))
        mv1, mv2, mv3, mv4 = (sb(f"mv{n}", [P, TILES, 2]) for n in range(1, 5))
        X0_PART = 1
        vv1, rs1 = sb("vv1", [P, 2, TILES]), sb("rs1", [P, 2, TILES])
        vv2, vv3, vv4, rs2, rs3, rs4 = (sb(n, [P, TILES]) for n in ("vv2", "vv3", "vv4", "rs2", "rs3", "rs4"))
        power = sb("power", [P, 2, TILES])
        Z1, Z2, Z4 = (sb(f"Z{n}", [P, TILES, WIDTH]) for n in (1, 2, 4))
        z1_h, z2_h, z1_l, z2_l = (sb(n, [P, GROUP], F32R) for n in ("z1_h", "z2_h", "z1_l", "z2_l"))
        z4_t = sb("z4_t", [P, GROUP])
        Y3, YG, YS, YB, YC = (sb(n, [P, TILES, WIDTH]) for n in ("Y3", "YG", "YS", "YB", "YC"))
        U3 = [sb(f"U3{s}", [P, TILES, WIDTH]) for s in range(STREAMS)]
        q_in, k_in, v_in, xo_in, th = (sb(n, [P, TILES, P]) for n in ("q_in", "k_in", "v_in", "xo_in", "th"))
        qd = sb("qd", [P, TILES, P])
        qx = sb("qx", [P, QUAD, TILES, P])
        kx = sb("kx", [P, TILES * CHUNKS, QUAD, CHUNK])
        kt = sb("kt", [P, TILES, WIDTH])
        vt = sb("vt", [P, TILES, WIDTH])
        vh = sb("vh", [P, TILES, WIDTH])
        vx = sb("vx", [P, TILES, CHUNKS, QUAD, CHUNK])
        S = [sb(f"S{n}", [P, HALVES * S_HALF]) for n in range(2)]
        gate = sb("gate", [P, TILES, P])
        gated = sb("gated", [P, TILES, P])
        state = sb("state", [P, LAYERS, STREAMS, TILES, WIDTH])
        state_sum = sb("state_sum", [P, TILES, WIDTH])
        half_state = sb("half_state", [P, TILES, WIDTH])
        hid = sb("hid", [P, HC, TILES, P])

        R = [bank(f"R{n}") for n in range(3)]
        RET = bank("RET")
        M = bank("M")
        F = [bank(f"F{n}") for n in range(2)]
        F2 = bank("F2")

        params = sem("params")
        x_in = [sem(f"x_in{s}") for s in range(STREAMS)]
        stored = [sem(f"stored{s}") for s in range(STREAMS)]
        zeroed = sem("zeroed")
        prep = sem("prep")
        prep_pe = sem("prep_pe")
        prep_act = sem("prep_act")
        rs1_ok, rs2_ok, rs3_ok, rs4_ok = (sem(f"rs{n}_ok") for n in range(1, 5))
        ln1, z1_ok, z1_t, z1_hok, z1_lok = (sem(n) for n in ("ln1", "z1_ok", "z1_t", "z1_hok", "z1_lok"))
        ln2, z2_ok, z2_t, z2_hok, z2_lok = (sem(n) for n in ("ln2", "z2_ok", "z2_t", "z2_hok", "z2_lok"))
        projected, proj_out = sem("projected"), sem("proj_out")
        kt_ok, qd_ok, kx_act, kx_dve, qx_ok, x0_ok = (
            sem(n) for n in ("kt_ok", "qd_ok", "kx_act", "kx_dve", "qx_ok", "x0_ok"))
        tm_t, tm_out, vx_ok = sem("tm_t"), sem("tm_out"), sem("vx_ok")
        scored, masked, ret_done = sem("scored"), sem("masked"), sem("ret_done")
        half_summed, half_ok = sem("half_summed"), sem("half_ok")
        summed, sum_out, state_ok = sem("summed"), sem("sum_out"), sem("state_ok")
        gate_ok, gated_ok, reto_done, res1 = (sem(n) for n in ("gate_ok", "gated_ok", "reto_done", "res1"))
        xb1, xb2 = sem("xb1"), sem("xb2")
        ffn1_done, gelu_ok, ffn2_done, res2 = (sem(n) for n in ("ffn1_done", "gelu_ok", "ffn2_done", "res2"))
        ln3, y3_ok, yg_ok, u3_ok, ln4, z4_ok, z4_tt, z4_tok = (
            sem(n) for n in ("ln3", "y3_ok", "yg_ok", "u3_ok", "ln4", "z4_ok", "z4_tt", "z4_tok"))
        signed, ys_ok, yb_ok, yc_ok, out_ok, xrb_ok = (
            sem(n) for n in ("signed", "ys_ok", "yb_ok", "yc_ok", "out_ok", "xrb_ok"))

        ident = con[:, C_ID:C_ID + P]
        PARAMS_IN = 16 * 8
        PREP = 14
        IDENTITY = ACT.Identity
        KX_ACT = 2

        def over_tiles(ap):
            return ap.unsqueeze(1).to_broadcast([P, TILES, ap.shape[-1]])

        def run(eng, play):
            play(Turn(0, -1), True, False, False, False)
            for c in range(PHASES):
                play(Turn(0, c), True, True, c == 3, False)
            with eng.Fori(1, STEPS - 1) as i:
                for c in range(PHASES):
                    play(Turn(i, c), True, True, c in (0, 3), c in (0, 1))
            last = STEPS - 1
            for c in range(PHASES):
                play(Turn(last, c), c < PHASES - 1, True, c in (0, 3), c in (0, 1))
            play(Turn(last, PHASES), False, False, True, True)
            play(Turn(last, PHASES + 1), False, False, False, True)

        block = ctx.enter_context(nc.Block())

        @block.sync
        def _(sp):
            for s in range(STREAMS):
                sp.dma_start(xin[s][:, :, :], x_v[s, 0]).then_inc(x_in[s], 16)
            sp.dma_start(col[:, :], columns).then_inc(params, 16)
            sp.dma_start(row[:, :, :], rows.partition_broadcast(P)).then_inc(params, 16)
            sp.dma_start(con[:, :], consts).then_inc(params, 16)
            sp.dma_start(wp[:, :, :], proj_w.rearrange("l p n -> p l n")).then_inc(params, 16)
            sp.dma_start(w1[:, :, :], ffn1_w.rearrange("l p n -> p l n")).then_inc(params, 16)
            sp.dma_start(wo_in[:, :, :], reto_w.rearrange("l p n -> p l n")).then_inc(params, 16)
            sp.dma_start(w2[:, :, :, :], ffn2_w.rearrange("l (c p) n -> p l c n", p=P)).then_inc(params, 16)
            sp.dma_start(ws_in[:, :], sign_w).then_inc(params, 16)

            def loads(i):
                r = Turn(i, STREAMS - 1)
                sp.wait_ge(x0_ok, r.group(1, 1))
                sp.wait_ge(xrb_ok, r.group(1, 1))
                for s in range(STREAMS):
                    sp.dma_start(xin[s][:, :, :], x_v[s, 1:][i]).then_inc(x_in[s], 16)

            with sp.Fori(0, STEPS - 1) as i:
                loads(i)
                sp.wait_ge(out_ok, Turn(i, STREAMS - 1).group(1, 1))
                for s in reversed(range(STREAMS)):
                    sp.dma_start(out_v[s, i], OUT[s][:, :, :]).then_inc(stored[s], 16)
            for s in range(STREAMS):
                sp.wait_ge(out_ok, Turn(STEPS - 1, s).group(1, 1))
                sp.dma_start(out_v[s, STEPS - 1], OUT[s][:, :, :]).then_inc(stored[s], 16)
            for s in range(STREAMS):
                sp.wait_ge(stored[s], 16 * STEPS)

        @block.tensor
        def _(pe):
            def split_product(dst, w_h, w_l, z_h, z_l, low_ok, value):
                nc.tensor.matmul(dst, w_h, z_h, start=True, stop=False)
                nc.tensor.matmul(dst, w_l, z_h, start=False, stop=False)
                pe.wait_ge(low_ok, value)
                return nc.tensor.matmul(dst, w_h, z_l, start=False, stop=True)

            def transposes(dst, src):
                for t in range(TILES):
                    last = nc.tensor.transpose(dst[:, t * P:(t + 1) * P], src[:, t, :], ident)
                return last

            def z1_transposes(r):
                pe.wait_ge(z1_ok, r.count(1, 1))
                if r.past():
                    pe.wait_ge(z1_lok, r.count(1, 0))
                if r.past(3):
                    pe.wait_ge(gelu_ok, r.count(HC, -HC))
                transposes(F[1], Z1).then_inc(z1_t, 1)

            def play(s, has_r, has_f, has_o, has_tail):
                r, f, o = s.after(1), s, s.after(-1)
                st, ly, fly = r.stream, r.layer, f.layer

                def project():
                    for n in range(OUTS):
                        if n == 0:
                            pe.wait_ge(z1_hok, r.count(1, 1))
                            if r.past():
                                pe.wait_ge(masked, r.count(HALVES * TILES, -1))
                        elif n == 1:
                            if r.past():
                                pe.wait_ge(masked, r.count(HALVES * TILES, 0))
                        elif n == 2:
                            if r.past():
                                pe.wait_ge(masked, r.count(HALVES * TILES, -2))
                        else:
                            pe.wait_ge(proj_out, r.count(OUTS, 1))
                        w = slice(n * P, (n + 1) * P)
                        split_product(R[n % 3][:, :], wp_h[:, ly, w], wp_l[:, ly, w], z1_h[:, :], z1_l[:, :],
                                      z1_lok, r.count(1, 1)).then_inc(projected, 1)

                def token_major():
                    pe.wait_ge(proj_out, r.count(OUTS, 2))
                    transposes(R[1], k_in).then_inc(tm_t, 1)
                    pe.wait_ge(proj_out, r.count(OUTS, 3))
                    transposes(R[2], v_in).then_inc(tm_t, 1)

                def z2_transposes():
                    pe.wait_ge(z2_ok, f.count(1, 1))
                    if f.past():
                        pe.wait_ge(res2, f.count(1, 0))
                    transposes(F2, Z2).then_inc(z2_t, 1)

                def ffn1(n):
                    if n == 0:
                        pe.wait_ge(z2_hok, f.count(1, 1))
                    if n == 1:
                        pe.wait_ge(z1_lok, f.count(1, 2) if has_r else f.count(1, 1))
                    if n >= 2 or f.past():
                        pe.wait_ge(gelu_ok, f.count(HC, n - 1))
                    w = slice(n * P, (n + 1) * P)
                    split_product(F[n % 2][:, :], w1_h[:, fly, w], w1_l[:, fly, w], z2_h[:, :], z2_l[:, :],
                                  z2_lok, f.count(1, 1)).then_inc(ffn1_done, 1)

                def sums():
                    pe.wait_ge(kt_ok, r.count(1, 1))
                    pe.wait_ge(tm_out, r.count(2, 2))
                    if last_out is not None:
                        pe.wait_ge(ys_ok, last_out)
                    if r.past():
                        pe.wait_ge(half_ok, r.count(1, 0))
                    for t in range(TILES):
                        mm = nc.tensor.matmul(M[:, t * P:(t + 1) * P], kt[:, t, :], vh[:, t, :],
                                              start=True, stop=True, skip_group_check=True)
                    mm.then_inc(half_summed, 1)
                    for t in range(TILES):
                        mm = nc.tensor.matmul(R[2][:, t * P:(t + 1) * P], kt[:, t, :], vt[:, t, :],
                                              start=True, stop=True, skip_group_check=True)
                    mm.then_inc(summed, 1)

                def z4_transposes():
                    pe.wait_ge(z4_ok, o.group(1, 1))
                    if has_r:
                        pe.wait_ge(half_ok, r.count(1, 1))
                    elif last_out is not None:
                        pe.wait_ge(ys_ok, last_out)
                    transposes(M, Z4).then_inc(z4_tt, 1)

                def last_product():
                    pe.wait_ge(z4_tok, o.group(1, 1))
                    for t in range(TILES):
                        mm = nc.tensor.matmul(M[:, t * P:(t + 1) * P], z4_t[:, t * P:(t + 1) * P], ws[:, :],
                                              start=True, stop=True, skip_group_check=True)
                    mm.then_inc(signed, 1)

                def scores(t):
                    for h in range(HALVES):
                        n = HALVES * t + h
                        if n == 0:
                            pe.wait_ge(qx_ok, r.count(1, 1))
                            pe.wait_ge(kx_act, r.count(1, 1))
                            pe.wait_ge(kx_dve, r.count(1, 1))
                            pe.wait_ge(proj_out, r.count(OUTS, 4))
                        elif n == 1:
                            pe.wait_ge(kt_ok, r.count(1, 1))
                        elif n == 2:
                            pe.wait_ge(sum_out, r.count(1, 1))
                        else:
                            pe.wait_ge(masked, r.count(HALVES * TILES, n - 2))
                        for c in range(h * CHUNKS // HALVES, (h + 1) * CHUNKS // HALVES):
                            at, w = S_AT[c] - h * S_HALF, DEPTH[c]
                            mm = nc.tensor.matmul(
                                R[n % 3][:, at:at + QUAD * w].rearrange("p (g n) -> p g n", g=QUAD),
                                kx[:, t * CHUNKS + c, :, :], qx[:, :, t, c * CHUNK:c * CHUNK + w],
                                start=True, stop=True, skip_group_check=True)
                        mm.then_inc(scored, 1)

                def retention(t):
                    if t == 0:
                        if r.past():
                            pe.wait_ge(res1, r.count(1, 0))
                        if r.past(PHASES):
                            pe.wait_ge(state_ok, r.count(1, 1 - PHASES))
                        pe.wait_ge(vx_ok, r.count(1, 1))
                        pe.wait_ge(half_ok, r.count(1, 1))
                        pe.wait_ge(qd_ok, r.count(1, 1))
                    pe.wait_ge(masked, r.count(HALVES * TILES, HALVES * (t + 1)))
                    nc.tensor.matmul(RET[:, t * P:(t + 1) * P], state[:, ly, st, t, :], qd[:, t, :],
                                     start=True, stop=False, skip_group_check=True)
                    nc.tensor.matmul(RET[:, t * P + HALF:(t + 1) * P], half_state[:, t, :], qd[:, t, HALF:P],
                                     start=False, stop=False, skip_group_check=True)
                    for c in range(CHUNKS):
                        w = DEPTH[c]
                        for g in range(QUAD):
                            at = S_AT[c] + g * w
                            mm = nc.tensor.matmul(
                                RET[g * CHUNK:(g + 1) * CHUNK, t * P + c * CHUNK:t * P + c * CHUNK + w],
                                vx[:, t, c, g, :], S[t % 2][:, at:at + w],
                                start=False, stop=(c == CHUNKS - 1), skip_group_check=True)
                    mm.then_inc(ret_done, 1)

                def ffn2(t):
                    if t == 0:
                        pe.wait_ge(gelu_ok, f.count(HC, HC))
                        pe.wait_ge(z2_lok, f.count(1, 1))
                    for c in range(HC):
                        mm = nc.tensor.matmul(F2[:, t * P:(t + 1) * P], hid[:, c, t, :], w2[:, fly, c, :],
                                              start=(c == 0), stop=(c == HC - 1), skip_group_check=True)
                    if t == TILES - 1:
                        mm.then_inc(ffn2_done, 1)

                def output_projection():
                    pe.wait_ge(gated_ok, r.count(1, 1))
                    for t in range(TILES):
                        mm = nc.tensor.matmul(RET[:, t * P:(t + 1) * P], gated[:, t, :], wo[:, ly, :],
                                              start=True, stop=True, skip_group_check=True)
                    mm.then_inc(reto_done, 1)

                if s.c in (0, 3):
                    last_out = o.group(1, 0) if o.past_groups() else None
                elif s.c == 1:
                    last_out = Turn(s.i, -1).group(1, 1) if Turn(s.i, 3 - PHASES).past(3) else None
                else:
                    last_out = None
                if has_r:
                    project()
                    token_major()
                if has_f:
                    z2_transposes()
                    ffn1(0)
                    ffn1(1)
                if has_r:
                    sums()
                if has_f:
                    ffn1(2)
                    ffn1(3)
                if has_r:
                    scores(0)
                if has_f:
                    for t in range(TILES):
                        ffn2(t)
                if has_r:
                    scores(1)
                    retention(0)
                    scores(2)
                    retention(1)
                    scores(3)
                    retention(2)
                if has_o:
                    z4_transposes()
                if has_r:
                    retention(3)
                    if not r.final:
                        z1_transposes(r.after(1))
                if has_o:
                    last_product()
                if has_r:
                    output_projection()

            pe.wait_ge(params, PARAMS_IN)
            for n in range(LAYERS * OUTS):
                nc.tensor.matmul(F[0][:, n:n + 1], wp[:, n // OUTS, n % OUTS * P:(n % OUTS + 1) * P],
                                 col[:, COL_B1 + n // OUTS:COL_B1 + n // OUTS + 1],
                                 start=True, stop=True, skip_group_check=True)
            for n in range(LAYERS * HC):
                mm = nc.tensor.matmul(F[0][:, 16 + n:17 + n], w1[:, n // HC, n % HC * P:(n % HC + 1) * P],
                                      col[:, COL_B2 + n // HC:COL_B2 + n // HC + 1],
                                      start=True, stop=True, skip_group_check=True)
            mm.then_inc(prep_pe, 1)
            z1_transposes(Turn(0, 0))
            pe.wait_ge(prep, PREP)
            run(pe, play)

        @block.scalar
        def _(act):
            def high_part(dst, src):
                return nc.scalar.activation(dst, src, ACT.Copy)

            def z1_high(r):
                act.wait_ge(z1_t, r.count(1, 1))
                if r.past():
                    act.wait_ge(projected, r.count(OUTS, 0))
                high_part(z1_h[:, :], F[1][:, :]).then_inc(z1_hok, 1)

            def by_tile(ap):
                return ap.rearrange("p (t n) -> p t n", t=TILES)

            def play(s, has_r, has_f, has_o, has_tail):
                r, f, o = s.after(1), s, s.after(-1)
                ly, fly = r.layer, f.layer

                def projections():
                    for n, dst in enumerate((q_in, k_in, v_in, xo_in)):
                        act.wait_ge(projected, r.count(OUTS, n + 1))
                        if r.past():
                            if n == 0:
                                act.wait_ge(qd_ok, r.count(1, 0))
                            elif n == 1:
                                act.wait_ge(tm_t, r.count(2, -1))
                                act.wait_ge(kx_dve, r.count(1, 0))
                            elif n == 2:
                                act.wait_ge(tm_t, r.count(2, 0))
                            else:
                                act.wait_ge(gate_ok, r.count(1, 0))
                        bias = pbias[:, ly * OUTS + n:ly * OUTS + n + 1]
                        src = by_tile(R[n % 3][:, :])
                        ins = nc.scalar.activation(dst[:, :, :], src, IDENTITY, bias=bias)
                        if n == 3:
                            ins = nc.scalar.activation(th[:, :, :], src, ACT.Tanh, scale=0.5, bias=hbias[:, ly:ly + 1])
                        ins.then_inc(proj_out, 1)

                def queries(g):
                    if g == 0:
                        act.wait_ge(proj_out, r.count(OUTS, 1))
                        if r.past():
                            act.wait_ge(scored, r.count(HALVES * TILES, 0))
                    rows_g = slice(g * CHUNK, (g + 1) * CHUNK)
                    ins = nc.scalar.copy(qx[rows_g, g, :, :], q_in[rows_g, :, :])
                    if g == QUAD - 1:
                        ins.then_inc(qx_ok, 1)

                def keys(j):
                    if j == 0:
                        act.wait_ge(proj_out, r.count(OUTS, 2))
                    ins = nc.scalar.activation(kx[:, :, j, :], k_in[:, :, :].rearrange("p t (c n) -> p (t c) n", c=CHUNKS),
                                               ACT.Copy, scale=con[:, C_JM + j:C_JM + j + 1])
                    if j == KX_ACT - 1:
                        ins.then_inc(kx_act, 1)

                def values():
                    act.wait_ge(tm_t, r.count(2, 2))
                    if r.past():
                        act.wait_ge(summed, r.count(1, 0))
                    nc.scalar.activation(vt[:, :, :], by_tile(R[2][:, :]), ACT.Copy).then_inc(tm_out, 1)
                    nc.scalar.activation(vh[0:HALF, :, :], by_tile(R[2][0:HALF, :]), ACT.Copy).then_inc(tm_out, 1)

                def spread_values(c):
                    if c == 0:
                        act.wait_ge(tm_out, r.count(2, 1))
                        if r.past():
                            act.wait_ge(ret_done, r.count(TILES, 0))
                    v = vt[c * CHUNK:(c + 1) * CHUNK, :, :].rearrange("p t (g j e) -> p t g j e", g=QUAD, j=QUAD)
                    for j in range(QUAD):
                        ins = nc.scalar.copy(
                            vx[j * CHUNK:(j + 1) * CHUNK, :, c, :, j * DH:(j + 1) * DH], v[:, :, :, j, :])
                    if c == CHUNKS - 1:
                        ins.then_inc(vx_ok, 1)

                def z2_high():
                    act.wait_ge(z2_t, f.count(1, 1))
                    if f.past():
                        act.wait_ge(ffn1_done, f.count(HC, 0))
                    high_part(z2_h[:, :], F2[:, :]).then_inc(z2_hok, 1)

                def gelu(n):
                    act.wait_ge(ffn1_done, f.count(HC, n + 1))
                    if n == 0 and f.past():
                        act.wait_ge(ffn2_done, f.count(1, 0))
                    nc.scalar.activation(hid[:, n, :, :], by_tile(F[n % 2][:, :]), ACT.Gelu,
                                         bias=f1bias[:, fly * HC + n:fly * HC + n + 1]).then_inc(gelu_ok, 1)

                if has_r:
                    projections()
                    queries(0)
                if has_f:
                    z2_high()
                if has_r:
                    values()
                    keys(0)
                if has_f:
                    gelu(0)
                if has_r:
                    keys(1)
                    queries(1)
                if has_f:
                    gelu(1)
                if has_r:
                    queries(2)
                    queries(3)
                if has_f:
                    gelu(2)
                    gelu(3)
                if has_r:
                    for c in range(CHUNKS):
                        spread_values(c)
                if has_o:
                    act.wait_ge(z4_tt, o.group(1, 1))
                    if o.past_groups():
                        act.wait_ge(signed, o.group(1, 0))
                    nc.scalar.activation(z4_t[:, :], M[:, :], ACT.Copy).then_inc(z4_tok, 1)
                if has_r and not r.final:
                    z1_high(r.after(1))

            z1_high(Turn(0, 0))
            act.wait_ge(prep, PREP)
            act.wait_ge(zeroed, 1)
            run(act, play)

        @block.vector
        def _(dve):
            def statistics(src, st, mv, chain, value):
                for t in range(TILES):
                    ins = nc.vector.bn_stats(st[:, t, :], src[:, t, :])
                ins.then_inc(chain, 1)
                dve.wait_ge(chain, value(1))
                nc.vector.memset(idle[:, :], 0.0)
                for t in range(TILES):
                    ins = nc.vector.bn_aggr(mv[:, t, :], st[:, t, :])
                ins.then_inc(chain, 1)
                dve.wait_ge(chain, value(2))

            def normalise(dst, src, mv, rs):
                for t in range(TILES):
                    ins = nc.vector.tensor_scalar(dst[:, t, :], src[:, t, :], mv[:, t, 0:1], rs[:, t:t + 1],
                                                  ALU.subtract, ALU.mult)
                return ins

            def shifted(dst, mv):
                return nc.vector.tensor_scalar(dst, mv[:, :, 1], EPS, None, ALU.add)

            def first_norm(r):
                st = r.stream
                if r.layer == 0:
                    dve.wait_ge(x_in[st], r.step(16, 16))
                    statistics(xin[st], st1, mv1, ln1, lambda k: r.count(3, k))
                    shifted(vv1[:, X0_PART, :], mv1)
                    nc.vector.tensor_scalar(vv1[:, 0, :], mv1[:, :, 1], 1.0 + EPS, EPS * EPS,
                                            ALU.mult, ALU.add).then_inc(ln1, 1)
                else:
                    dve.wait_ge(res2, r.count(1, -1))
                    statistics(X[st], st1, mv1, ln1, lambda k: r.count(3, k))
                    shifted(vv1[:, 0, :], mv1).then_inc(ln1, 1)

            def first_normalise(r):
                dve.wait_ge(rs1_ok, r.count(1, 1))
                if r.past():
                    dve.wait_ge(z1_t, r.count(1, 0))
                src = X[r.stream] if r.layer else xin[r.stream]
                normalise(Z1, src, mv1, rs1[:, 0, :]).then_inc(z1_ok, 1)

            def input_normalise(r):
                if r.layer == 0:
                    normalise(X[r.stream], xin[r.stream], mv1, rs1[:, X0_PART, :]).then_inc(x0_ok, 1)

            def low_part(r, dst, src, high, sem_h, sem_l):
                dve.wait_ge(sem_h, r.count(1, 1))
                nc.vector.tensor_tensor(dst[:, :], src[:, :], high[:, :].bitcast(F32), ALU.subtract).then_inc(sem_l, 1)

            def by_tile(ap):
                return ap.rearrange("p (t n) -> p t n", t=TILES)

            def play(s, has_r, has_f, has_o, has_tail):
                r, f, o = s.after(1), s, s.after(-1)
                st, ly, fst, ost = r.stream, r.layer, f.stream, o.stream

                def add_retention():
                    dve.wait_ge(reto_done, f.count(1, 1))
                    dve.wait_ge(xb1, f.count(1, 1))
                    nc.vector.tensor_tensor(X[fst][:, :, :], by_tile(RET[:, :]), X[fst][:, :, :],
                                            ALU.add).then_inc(res1, 1)

                def second_norm():
                    dve.wait_ge(res1, f.count(1, 1))
                    statistics(X[fst], st2, mv2, ln2, lambda k: f.count(3, k))
                    shifted(vv2[:, :], mv2).then_inc(ln2, 1)

                def second_normalise():
                    dve.wait_ge(rs2_ok, f.count(1, 1))
                    if f.past():
                        dve.wait_ge(z2_t, f.count(1, 0))
                    normalise(Z2, X[fst], mv2, rs2).then_inc(z2_ok, 1)

                def add_feed_forward():
                    dve.wait_ge(ffn2_done, f.count(1, 1))
                    dve.wait_ge(xb2, f.count(1, 1))
                    dst = XO if f.layer == LAYERS - 1 else X
                    nc.vector.tensor_tensor(dst[fst][:, :, :], by_tile(F2[:, :]), X[fst][:, :, :],
                                            ALU.add).then_inc(res2, 1)

                def decayed_queries():
                    dve.wait_ge(proj_out, r.count(OUTS, 1))
                    if r.past():
                        dve.wait_ge(ret_done, r.count(TILES, 0))
                    nc.vector.tensor_tensor(qd[:, :, :], q_in[:, :, :], over_tiles(con[:, C_DQ:C_DQ + P]),
                                            ALU.mult).then_inc(qd_ok, 1)

                def keys_by_token():
                    dve.wait_ge(tm_t, r.count(2, 1))
                    if r.past():
                        dve.wait_ge(summed, r.count(1, 0))
                    nc.vector.tensor_tensor(kt[:, :, :], by_tile(R[1][:, :]), over_tiles(con[:, C_DK:C_DK + P]),
                                            ALU.mult).then_inc(kt_ok, 1)

                def keys():
                    dve.wait_ge(proj_out, r.count(OUTS, 2))
                    if r.past():
                        dve.wait_ge(scored, r.count(HALVES * TILES, 0))
                    k = k_in[:, :, :].rearrange("p t (c n) -> p (t c) n", c=CHUNKS)
                    for j in range(KX_ACT, QUAD):
                        ins = nc.vector.tensor_scalar(kx[:, :, j, :], k, con[:, C_JM + j:C_JM + j + 1], None, ALU.mult)
                    ins.then_inc(kx_dve, 1)

                def gates():
                    dve.wait_ge(proj_out, r.count(OUTS, 4))
                    if r.past():
                        dve.wait_ge(gated_ok, r.count(1, 0))
                    nc.vector.scalar_tensor_tensor(out=gate[:, :, :], in0=th[:, :, :], scalar=1.0, in1=xo_in[:, :, :],
                                                   op0=ALU.add, op1=ALU.mult).then_inc(gate_ok, 1)

                def half_sums():
                    dve.wait_ge(half_summed, r.count(1, 1))
                    if r.past():
                        dve.wait_ge(ret_done, r.count(TILES, 0))
                    nc.vector.tensor_tensor(half_state[:, :, :], by_tile(M[:, :]), over_tiles(con[:, C_BM:C_BM + P]),
                                            ALU.mult).then_inc(half_ok, 1)

                def whole_sums():
                    dve.wait_ge(summed, r.count(1, 1))
                    if r.past():
                        dve.wait_ge(state_ok, r.count(1, 0))
                    nc.vector.tensor_tensor(state_sum[:, :, :], by_tile(R[2][:, :]), state[:, ly, st, :, :],
                                            ALU.add).then_inc(sum_out, 1)

                def mask(t):
                    if t >= 2 or r.past():
                        dve.wait_ge(ret_done, r.count(TILES, t - 1))
                    for h in range(HALVES):
                        n = HALVES * t + h
                        dve.wait_ge(scored, r.count(HALVES * TILES, n + 1))
                        nc.vector.tensor_tensor(S[t % 2][:, h * S_HALF:(h + 1) * S_HALF], R[n % 3][:, 0:S_HALF],
                                                con[:, C_CM:C_CM + S_HALF], ALU.mult).then_inc(masked, 1)

                def apply_gates():
                    dve.wait_ge(ret_done, r.count(TILES, TILES))
                    dve.wait_ge(gate_ok, r.count(1, 1))
                    if r.past():
                        dve.wait_ge(reto_done, r.count(1, 0))
                    nc.vector.tensor_tensor(gated[:, :, :], by_tile(RET[:, :]), gate[:, :, :],
                                            ALU.mult).then_inc(gated_ok, 1)

                def final_norm():
                    dve.wait_ge(res2, o.count(1, 1))
                    statistics(XO[ost], st3, mv3, ln3, lambda k: o.group(3, k))
                    shifted(vv3[:, :], mv3).then_inc(ln3, 1)

                def final_normalise():
                    dve.wait_ge(rs3_ok, o.group(1, 1))
                    if o.past_groups():
                        dve.wait_ge(yg_ok, o.group(1, 0))
                    normalise(Y3, XO[ost], mv3, rs3).then_inc(y3_ok, 1)

                def last_norm():
                    dve.wait_ge(u3_ok, o.group(1, 1))
                    statistics(U3[ost], st4, mv4, ln4, lambda k: o.group(3, k))
                    shifted(vv4[:, :], mv4).then_inc(ln4, 1)

                def last_normalise():
                    dve.wait_ge(rs4_ok, o.group(1, 1))
                    if o.past_groups():
                        dve.wait_ge(z4_tt, o.group(1, 0))
                    normalise(Z4, U3[ost], mv4, rs4).then_inc(z4_ok, 1)

                def scale_last():
                    dve.wait_ge(signed, o.group(1, 1))
                    if o.past_groups():
                        dve.wait_ge(yb_ok, o.group(1, 0))
                    nc.vector.tensor_tensor(YS[:, :, :], by_tile(M[:, :]), over_tiles(row[:, ROW_SC, :]),
                                            ALU.mult).then_inc(ys_ok, 1)

                if has_f:
                    add_retention()
                    second_norm()
                if has_r:
                    decayed_queries()
                if has_f:
                    second_normalise()
                if has_r:
                    keys_by_token()
                if has_f:
                    low_part(f, z2_l, F2, z2_h, z2_hok, z2_lok)
                if has_r:
                    keys()
                    half_sums()
                    whole_sums()
                    gates()
                if has_o:
                    final_norm()
                if has_r:
                    mask(0)
                if has_o:
                    final_normalise()
                if has_f:
                    add_feed_forward()
                if has_r:
                    if not r.final:
                        first_norm(r.after(1))
                    mask(1)
                if has_o:
                    last_norm()
                if has_r:
                    mask(2)
                    if not r.final:
                        first_normalise(r.after(1))
                    mask(3)
                    if not r.final:
                        input_normalise(r.after(1))
                if has_o:
                    last_normalise()
                if has_r:
                    apply_gates()
                    if not r.final:
                        dve.wait_ge(projected, r.count(OUTS, OUTS))
                        low_part(r.after(1), z1_l, F[1], z1_h, z1_hok, z1_lok)
                if has_o:
                    scale_last()

            first_norm(Turn(0, 0))
            first_normalise(Turn(0, 0))
            input_normalise(Turn(0, 0))
            dve.wait_ge(params, PARAMS_IN)
            for w, g, w_g in ((wp, COL_G1, wp_g), (w1, COL_G2, w1_g)):
                for n in range(LAYERS):
                    nc.vector.tensor_scalar(w_g[:, n, :], w[:, n, :], col[:, g + n:g + n + 1], None,
                                            ALU.mult).then_inc(prep, 1)
            dve.wait_ge(prep, 4)
            nc.vector.tensor_copy(wp_h[:, :, :], wp_g[:, :, :]).then_inc(prep, 1)
            nc.vector.tensor_copy(w1_h[:, :, :], w1_g[:, :, :]).then_inc(prep, 1)
            dve.wait_ge(prep, 6)
            nc.vector.tensor_tensor(wp_l[:, :, :], wp_g[:, :, :], wp_h[:, :, :].bitcast(F32), ALU.subtract).then_inc(prep, 1)
            nc.vector.tensor_tensor(w1_l[:, :, :], w1_g[:, :, :], w1_h[:, :, :].bitcast(F32), ALU.subtract).then_inc(prep, 1)
            nc.vector.tensor_scalar(wo[:, :, :], wo_in[:, :, :], 0.5, None, ALU.mult).then_inc(prep, 1)
            nc.vector.tensor_scalar(ws_ge[:, :], ws_in[:, :], 0.0, 2.0, ALU.is_ge, ALU.mult).then_inc(prep, 1)
            dve.wait_ge(prep, 10)
            nc.vector.tensor_scalar(ws[:, :], ws_ge[:, :], -1.0, None, ALU.add).then_inc(prep, 1)
            dve.wait_ge(prep_pe, 1)
            nc.vector.tensor_tensor(pbias[:, :], F[0][:, 0:LAYERS * OUTS], col[:, COL_PB:COL_PB + LAYERS * OUTS],
                                    ALU.add).then_inc(prep, 1)
            nc.vector.tensor_tensor(f1bias[:, :], F[0][:, 16:16 + LAYERS * HC], col[:, COL_F1B:COL_F1B + LAYERS * HC],
                                    ALU.add).then_inc(prep, 1)
            dve.wait_ge(prep, 13)
            nc.vector.tensor_scalar(hbias[:, :], pbias[:, :].rearrange("p (l o) -> p l o", o=OUTS)[:, :, OUTS - 1],
                                    0.5, None, ALU.mult).then_inc(prep, 1)
            low_part(Turn(0, 0), z1_l, F[1], z1_h, z1_hok, z1_lok)
            dve.wait_ge(zeroed, 1)
            run(dve, play)

        @block.gpsimd
        def _(pool):
            def add_row(dst, a, n, op=ALU.add):
                return nc.gpsimd.tensor_tensor(dst[:, :, :], a[:, :, :], over_tiles(row[:, n, :]), op)

            def inverse_root(dst, src, ready, value, done):
                pool.wait_ge(ready, value)
                nc.gpsimd.tensor_tensor(dst, src, power[:, 0:dst.shape[1], :] if len(dst.shape) == 3 else power[:, 0, :],
                                        ALU.pow).then_inc(done, 1)

            def carry_wait():
                nc.gpsimd.tensor_tensor(held[:, :], power[:, 0, 0:1], power[:, 0, 0:1], ALU.mult)

            def input_copy(r):
                st = r.stream
                pool.wait_ge(x_in[st], r.step(16, 16))
                if r.past_groups(STREAMS):
                    pool.wait_ge(u3_ok, r.group(1, -1))
                add_row(XRB[st], xin[st], ROW_LB).then_inc(xrb_ok, 1)

            def first_root(r):
                n = 1 if r.layer else 2
                inverse_root(rs1[:, 0:n, :], vv1[:, 0:n, :], ln1, r.count(3, 3), rs1_ok)

            def first_bias(r):
                if r.layer == 0:
                    pool.wait_ge(x0_ok, r.group(1, 1))
                else:
                    pool.wait_ge(z1_ok, r.count(1, 1))
                add_row(X[r.stream], X[r.stream], ROW_RB + r.layer).then_inc(xb1, 1)

            def play(s, has_r, has_f, has_o, has_tail):
                r, f, o = s.after(1), s, s.after(-1)
                st, ly, ost = r.stream, r.layer, o.stream

                def residual_input():
                    pool.wait_ge(y3_ok, o.group(1, 1))
                    add_row(YG, Y3, ROW_LG, ALU.mult).then_inc(yg_ok, 1)
                    pool.wait_ge(yg_ok, o.group(1, 1))
                    pool.wait_ge(xrb_ok, o.group(1, 1))
                    nc.gpsimd.tensor_tensor(U3[ost][:, :, :], YG[:, :, :], XRB[ost][:, :, :],
                                            ALU.add).then_inc(u3_ok, 1)
                    if not (isinstance(s.i, int) and s.i == STEPS - 1 and s.c > 0):
                        input_copy(o.after(2))

                def output(o):
                    pool.wait_ge(ys_ok, o.group(1, 1))
                    add_row(YB, YS, ROW_BI).then_inc(yb_ok, 1)
                    pool.wait_ge(yb_ok, o.group(1, 1))
                    carry_wait()
                    nc.gpsimd.tensor_scalar(YC[:, :, :], YB[:, :, :], CLIP, -CLIP, ALU.min, ALU.max).then_inc(yc_ok, 1)
                    pool.wait_ge(yc_ok, o.group(1, 1))
                    if o.past_groups(STREAMS):
                        pool.wait_ge(stored[o.stream], o.step(16, 0))
                    nc.gpsimd.tensor_tensor(OUT[o.stream][:, :, :], YC[:, :, :], U3[o.stream][:, :, :],
                                            ALU.add).then_inc(out_ok, 1)

                if has_f:
                    inverse_root(rs2[:, :], vv2[:, :], ln2, f.count(3, 3), rs2_ok)
                    pool.wait_ge(z2_ok, f.count(1, 1))
                    add_row(X[f.stream], X[f.stream], ROW_F2B + f.layer).then_inc(xb2, 1)
                if has_o:
                    inverse_root(rs3[:, :], vv3[:, :], ln3, o.group(3, 3), rs3_ok)
                    residual_input()
                if has_r and not r.final:
                    first_root(r.after(1))
                if has_tail:
                    output(s.after(-2))
                if has_o:
                    inverse_root(rs4[:, :], vv4[:, :], ln4, o.group(3, 3), rs4_ok)
                if has_r:
                    if not r.final:
                        first_bias(r.after(1))
                    pool.wait_ge(sum_out, r.count(1, 1))
                    pool.wait_ge(ret_done, r.count(TILES, TILES))
                    nc.gpsimd.tensor_tensor(state[:, ly, st, :, :], state_sum[:, :, :],
                                            over_tiles(con[:, C_SM:C_SM + P]), ALU.mult).then_inc(state_ok, 1)

            nc.gpsimd.memset(power[:, :, :], -0.5)
            nc.gpsimd.memset(state[:, :, :, :, :], 0.0)
            nc.gpsimd.memset(qx[:, :, :, :], 0.0)
            nc.gpsimd.memset(vh[:, :, :], 0.0)
            nc.gpsimd.memset(vx[:, :, :, :, :], 0.0).then_inc(zeroed, 1)
            pool.wait_ge(zeroed, 1)
            pool.wait_ge(params, PARAMS_IN)
            for st in range(STREAMS):
                input_copy(Turn(0, st))
            first_root(Turn(0, 0))
            first_bias(Turn(0, 0))
            run(pool, play)


def constants():
    head = np.arange(P) // DH
    gamma = 1.0 - 2.0 ** (-5.0 - head.astype(np.float64))
    n = np.arange(P)
    con = np.zeros((P, CONSTS), np.float64)
    con[:, C_DQ:C_DQ + P] = gamma[:, None] ** n[None, :]
    con[:, C_DK:C_DK + P] = gamma[None, :] ** -n[:, None].astype(np.float64)
    con[:, C_BM:C_BM + P] = head[:, None] == head[None, :]
    con[:, C_SM:C_SM + P] = con[:, C_BM:C_BM + P] * gamma[:, None] ** P
    con[:, C_ID:C_ID + P] = np.eye(P)
    j, m = n // CHUNK, n % CHUNK
    decay = []
    for c in range(CHUNKS // HALVES):
        lag = np.arange(DEPTH[c])[None, :] - m[:, None]
        for g in range(QUAD):
            decay.append((lag >= 0) * gamma[(QUAD * g + j) * DH][:, None] ** np.maximum(lag, 0))
    con[:, C_CM:C_CM + S_HALF] = np.concatenate(decay, axis=1)
    con[:, C_JM:C_JM + QUAD] = (head[:, None] % QUAD) == np.arange(QUAD)[None, :]
    return con.astype(np.float32)


def kernel(**inputs):
    import concourse.bacc as bacc
    from concourse.bass_utils import run_bass_kernel_spmd

    a = {n: np.ascontiguousarray(v) for n, v in inputs.items()}

    def by_partition(v):
        return v.reshape(-1, P).T

    columns = np.concatenate([by_partition(a["L0_attn_" + n]) for n in (
        "ln1_g", "ln1_b", "ln2_g", "ln2_b", "proj_b", "ffn1_b")], axis=1)
    rows = np.concatenate([a[n].reshape(-1, WIDTH) for n in (
        "L0_attn_reto_b", "L0_attn_ffn2_b", "L0_attn_lnf_g", "L0_attn_lnf_b", "L0_ffn_scale", "L0_ffn_bias")], axis=0)
    arrays = {
        "x": a["L0_attn_x"], "columns": columns, "rows": rows, "consts": constants(),
        "proj_w": a["L0_attn_proj_w"], "reto_w": a["L0_attn_reto_w"], "ffn1_w": a["L0_attn_ffn1_w"],
        "ffn2_w": a["L0_attn_ffn2_w"], "sign_w": a["L0_ffn_weights"].T,
    }
    arrays = {n: np.ascontiguousarray(v) for n, v in arrays.items()}
    nc = bacc.Bacc("TRN2", target_bir_lowering=False, num_devices=1)
    args = [nc.dram_tensor(n + "_dram", v.shape, mybir.dt.from_np(v.dtype), kind="ExternalInput").ap()
            for n, v in arrays.items()]
    out = nc.dram_tensor("out_dram", arrays["x"].shape, F32, kind="ExternalOutput").ap()
    retention_ffn(nc, *args, out)
    r = run_bass_kernel_spmd(nc, [{n + "_dram": v for n, v in arrays.items()}], core_ids=[0])
    return r.results[0]["out_dram"]
```

```python
from contextlib import ExitStack

import numpy as np

import concourse.bass as bass
from concourse import mybir

P = 128
BATCH, LENGTH, WIDTH = 8, 1024, 128
HEADS, LAYERS, HIDDEN = 16, 2, 512
DH = WIDTH // HEADS
STREAMS = 2
TILES = BATCH // STREAMS
GROUP = TILES * P
STEPS = LENGTH // P
CHUNK = 32
CHUNKS = P // CHUNK
QUAD = 4
OUTS = 4
HC = HIDDEN // P
EPS = 1e-5
CLIP = 100.0
PHASES = 2 * LAYERS
HALVES = 2
HALF = P // HALVES
PAIR = 2
DEPTH = [HALF - c % (CHUNKS // HALVES) * CHUNK for c in range(CHUNKS)]
S_AT = [QUAD * sum(DEPTH[:c]) for c in range(CHUNKS)]
S_HALF = QUAD * sum(DEPTH) // HALVES

COL_G1, COL_B1, COL_G2, COL_B2 = 0, 2, 4, 6
COL_PB = 8
COL_F1B = COL_PB + LAYERS * OUTS
COLS = COL_F1B + LAYERS * HC
ROW_RB, ROW_F2B, ROW_LG, ROW_LB, ROW_SC, ROW_BI = 0, 2, 4, 5, 6, 7
ROWS = 8
C_DQ, C_DK, C_SM, C_BM, C_ID, C_CM = 0, P, 2 * P, 3 * P, 4 * P, 5 * P
C_JM = C_CM + S_HALF
CONSTS = C_JM + QUAD

F32 = mybir.dt.float32
F32R = mybir.dt.float32r
ALU = mybir.AluOpType
ACT = mybir.ActivationFunctionType


class Turn:

    def __init__(self, i, c):
        self.i, self.c = i, c

    def after(self, n):
        return Turn(self.i, self.c + n)

    @property
    def stream(self):
        return self.c % STREAMS

    @property
    def layer(self):
        return (self.c // STREAMS) % LAYERS

    def count(self, per, k=0):
        return self.i * (PHASES * per) + (per * self.c + k)

    def past(self, n=1):
        return not isinstance(self.i, int) or PHASES * self.i + self.c >= n

    def past_groups(self, n=1):
        return not isinstance(self.i, int) or self.group(1) >= n

    @property
    def last_time(self):
        return isinstance(self.i, int) and PHASES * self.i + self.c >= PHASES * (STEPS - 1)

    @property
    def final(self):
        return isinstance(self.i, int) and PHASES * self.i + self.c == PHASES * STEPS - 1

    def group(self, per, k=0):
        return self.i * (STREAMS * per) + (per * (self.c // PHASES * STREAMS + self.stream) + k)

    def step(self, per, k=0):
        return self.i * per + (per * (self.c // PHASES) + k)


def retention_ffn(nc, x, columns, rows, consts, proj_w, reto_w, ffn1_w, ffn2_w, sign_w, out):
    x_v = x.rearrange("(s j) (t p) d -> s t p j d", s=STREAMS, p=P)
    out_v = out.rearrange("(s j) (t p) d -> s t p j d", s=STREAMS, p=P)

    with ExitStack() as ctx:
        def sb(name, shape, dt=F32):
            return ctx.enter_context(nc.sbuf_tensor(name, shape, dt))

        def bank(name):
            return ctx.enter_context(nc.psum_tensor(name, [P, GROUP], F32))

        def sem(name):
            return ctx.enter_context(nc.semaphore(name))

        col = sb("col", [P, COLS])
        row = sb("row", [P, ROWS, WIDTH])
        con = sb("con", [P, CONSTS])
        wp = sb("wp", [P, LAYERS, OUTS * P])
        wp_g = sb("wp_g", [P, LAYERS, OUTS * P])
        wp_h = sb("wp_h", [P, LAYERS, OUTS * P], F32R)
        wp_l = sb("wp_l", [P, LAYERS, OUTS * P], F32R)
        w1 = sb("w1", [P, LAYERS, HIDDEN])
        w1_g = sb("w1_g", [P, LAYERS, HIDDEN])
        w1_h = sb("w1_h", [P, LAYERS, HIDDEN], F32R)
        w1_l = sb("w1_l", [P, LAYERS, HIDDEN], F32R)
        w2 = sb("w2", [P, LAYERS, HC, WIDTH])
        wo_in = sb("wo_in", [P, LAYERS, WIDTH])
        wo = sb("wo", [P, LAYERS, WIDTH])
        ws_in = sb("ws_in", [P, WIDTH])
        ws_ge = sb("ws_ge", [P, WIDTH])
        ws = sb("ws", [P, WIDTH])
        pbias = sb("pbias", [P, LAYERS * OUTS])
        hbias = sb("hbias", [P, LAYERS])
        f1bias = sb("f1bias", [P, LAYERS * HC])
        xin = [sb(f"xin{s}", [P, TILES, WIDTH]) for s in range(STREAMS)]
        X = [sb(f"X{s}", [P, TILES, WIDTH]) for s in range(STREAMS)]
        XO = [sb(f"XO{s}", [P, TILES, WIDTH]) for s in range(STREAMS)]
        XRB = [sb(f"XRB{s}", [P, TILES, WIDTH]) for s in range(STREAMS)]
        OUT = [sb(f"OUT{s}", [P, TILES, WIDTH]) for s in range(STREAMS)]
        idle, held = sb("idle", [P, TILES // PAIR]), sb("held", [P, 1])
        st1, st2, st3, st4 = (sb(f"st{n}", [P, TILES, 6]) for n in range(1, 5))
        mv1, mv2, mv3, mv4 = (sb(f"mv{n}", [P, TILES, 2]) for n in range(1, 5))
        X0_PART = 1
        vv1, rs1 = sb("vv1", [P, 2, TILES]), sb("rs1", [P, 2, TILES])
        vv2, vv3, vv4, rs2, rs3, rs4 = (sb(n, [P, TILES]) for n in ("vv2", "vv3", "vv4", "rs2", "rs3", "rs4"))
        power = sb("power", [P, TILES])
        Z1, Z2, Z4 = (sb(f"Z{n}", [P, TILES, WIDTH]) for n in (1, 2, 4))
        z1_h, z2_h, z1_l, z2_l = (sb(n, [P, GROUP], F32R) for n in ("z1_h", "z2_h", "z1_l", "z2_l"))
        z4_t = sb("z4_t", [P, GROUP])
        Y3, YG, YS, YB, YC = (sb(n, [P, TILES, WIDTH]) for n in ("Y3", "YG", "YS", "YB", "YC"))
        U3 = [sb(f"U3{s}", [P, TILES, WIDTH]) for s in range(STREAMS)]
        q_in, k_in, v_in, xo_in, th = (sb(n, [P, TILES, P]) for n in ("q_in", "k_in", "v_in", "xo_in", "th"))
        qd = sb("qd", [P, TILES, P])
        qx = sb("qx", [P, QUAD, TILES, P])
        kx = sb("kx", [P, TILES * CHUNKS, QUAD, CHUNK])
        kt = sb("kt", [P, TILES, WIDTH])
        vt = sb("vt", [P, TILES, WIDTH])
        vx = sb("vx", [P, TILES, CHUNKS, QUAD, CHUNK])
        S = [sb(f"S{n}", [P, HALVES * S_HALF]) for n in range(2)]
        gate = sb("gate", [P, TILES, P])
        gated = sb("gated", [P, TILES, P])
        state = sb("state", [P, LAYERS, STREAMS, TILES, WIDTH])
        state_sum = sb("state_sum", [P, TILES, WIDTH])
        half_state = sb("half_state", [P, TILES, WIDTH])
        hid = sb("hid", [P, HC, TILES, P])

        R = [bank(f"R{n}") for n in range(3)]
        RET = bank("RET")
        M = bank("M")
        F = [bank(f"F{n}") for n in range(2)]
        F2 = bank("F2")

        first_params, params = sem("first_params"), sem("params")
        x_in = [sem(f"x_in{s}") for s in range(STREAMS)]
        stored = [sem(f"stored{s}") for s in range(STREAMS)]
        zeroed = sem("zeroed")
        prep = sem("prep")
        prep_pe = sem("prep_pe")
        prep_dve = sem("prep_dve")
        prep_pool = sem("prep_pool")
        rs0_ok = sem("rs0_ok")
        rs1_ok, rs2_ok, rs3_ok, rs4_ok = (sem(f"rs{n}_ok") for n in range(1, 5))
        ln1, z1_ok, z1_t, z1_hok, z1_lok = (sem(n) for n in ("ln1", "z1_ok", "z1_t", "z1_hok", "z1_lok"))
        ln2, z2_ok, z2_t, z2_hok, z2_lok = (sem(n) for n in ("ln2", "z2_ok", "z2_t", "z2_hok", "z2_lok"))
        projected, proj_out = sem("projected"), sem("proj_out")
        kt_ok, qd_ok, kx_act, kx_dve, qx_ok, x0_ok = (
            sem(n) for n in ("kt_ok", "qd_ok", "kx_act", "kx_dve", "qx_ok", "x0_ok"))
        tanh_ok = sem("tanh_ok")
        tm_t, vt_ok, vx_ok = sem("tm_t"), sem("vt_ok"), sem("vx_ok")
        scored, masked, ret_done = sem("scored"), sem("masked"), sem("ret_done")
        half_summed, half_ok = sem("half_summed"), sem("half_ok")
        summed, sum_out, state_ok = sem("summed"), sem("sum_out"), sem("state_ok")
        gate_ok, gated_ok, reto_done, res1 = (sem(n) for n in ("gate_ok", "gated_ok", "reto_done", "res1"))
        xb1, xb2 = sem("xb1"), sem("xb2")
        ffn1_done, gelu_ok, ffn2_done, res2 = (sem(n) for n in ("ffn1_done", "gelu_ok", "ffn2_done", "res2"))
        ln3, y3_ok, yg_ok, u3_ok, ln4, z4_ok, z4_tt, z4_tok = (
            sem(n) for n in ("ln3", "y3_ok", "yg_ok", "u3_ok", "ln4", "z4_ok", "z4_tt", "z4_tok"))
        signed, ys_ok, yb_ok, yc_ok, out_ok, xrb_ok = (
            sem(n) for n in ("signed", "ys_ok", "yb_ok", "yc_ok", "out_ok", "xrb_ok"))

        ident = con[:, C_ID:C_ID + P]
        FIRST_PARAMS_IN = 16 * 3
        PARAMS_IN = 16 * 5
        PREP_W, PREP_B, PREP_ALL = 1, 3, 10
        PREP_POOL = 2 * 3
        IDENTITY = ACT.Identity
        KX_DVE = 3

        def over_tiles(ap):
            return ap.unsqueeze(1).to_broadcast([P, TILES, ap.shape[-1]])

        def run(eng, play):
            play(Turn(0, -1), True, False, None, None, None)
            for c in range(PHASES):
                play(Turn(0, c), True, True, Turn(0, 2) if c == 3 else None, None, None)

            def turns(i, count):
                for c in range(PHASES):
                    play(Turn(i, c), c < count, True, *(
                        (None, Turn(i, -2), None), (Turn(i, -1), None, Turn(i, -2)),
                        (None, Turn(i, -1), None), (Turn(i, 2), None, Turn(i, -1)))[c])

            with eng.Fori(1, STEPS - 1) as i:
                turns(i, PHASES)
            last = STEPS - 1
            turns(last, PHASES - 1)
            play(Turn(last, PHASES), False, False, Turn(last, 3), Turn(last, 2), None)
            play(Turn(last, PHASES + 1), False, False, None, Turn(last, 3), Turn(last, 2))
            play(Turn(last, PHASES + 2), False, False, None, None, Turn(last, 3))

        block = ctx.enter_context(nc.Block())

        @block.sync
        def _(sp):
            sp.dma_start(xin[0][:, :, :], x_v[0, 0]).then_inc(x_in[0], 16)
            sp.dma_start(con[:, :], consts).then_inc(first_params, 16)
            sp.dma_start(wo_in[:, :, :], reto_w.rearrange("l p n -> p l n")).then_inc(params, 16)
            sp.dma_start(ws_in[:, :], sign_w).then_inc(params, 16)
            sp.dma_start(row[:, :, :], rows.partition_broadcast(P)).then_inc(params, 16)
            sp.dma_start(xin[1][:, :, :], x_v[1, 0]).then_inc(x_in[1], 16)

            def loads(i, ahead):
                before = Turn(i, PHASES * (ahead - 1) + STREAMS - 1)
                sp.wait_ge(x0_ok, before.group(1, 1))
                sp.wait_ge(xrb_ok, before.group(1, 1))
                for s in range(STREAMS):
                    sp.dma_start(xin[s][:, :, :], x_v[s, ahead:][i]).then_inc(x_in[s], 16)

            loads(0, 1)
            with sp.Fori(0, STEPS - 2) as i:
                loads(i, 2)
                sp.wait_ge(out_ok, Turn(i, STREAMS - 1).group(1, 1))
                for s in reversed(range(STREAMS)):
                    sp.dma_start(out_v[s, i], OUT[s][:, :, :]).then_inc(stored[s], 16)
            for t in range(STEPS - 2, STEPS):
                for s in range(STREAMS):
                    sp.wait_ge(out_ok, Turn(t, s).group(1, 1))
                    sp.dma_start(out_v[s, t], OUT[s][:, :, :]).then_inc(stored[s], 16)
            for s in range(STREAMS):
                sp.wait_ge(stored[s], 16 * (STEPS + 1))

        @block.tensor
        def _(pe):
            def bias(at, w, c):
                return nc.tensor.matmul(F[0][:, at:at + 1], w, col[:, c:c + 1],
                                        start=True, stop=True, skip_group_check=True)

            def other_biases():
                pe.wait_ge(params, PARAMS_IN)
                pe.wait_ge(prep, PREP_B)
                for n in range(OUTS, LAYERS * OUTS):
                    bias(n, wp[:, n // OUTS, n % OUTS * P:(n % OUTS + 1) * P], COL_B1 + n // OUTS)
                for n in range(LAYERS * HC):
                    mm = bias(LAYERS * OUTS + n, w1[:, n // HC, n % HC * P:(n % HC + 1) * P], COL_B2 + n // HC)
                mm.then_inc(prep_pe, 1)

            def high_passes(dst, w_h, w_l, z_h):
                nc.tensor.matmul(dst, w_h, z_h, start=True, stop=False)
                nc.tensor.matmul(dst, w_l, z_h, start=False, stop=False)

            def low_pass(dst, w_h, z_l):
                return nc.tensor.matmul(dst, w_h, z_l, start=False, stop=True)

            def transposes(dst, src, tiles=range(TILES)):
                for t in tiles:
                    last = nc.tensor.transpose(dst[:, t * P:(t + 1) * P], src[:, t, :], ident)
                return last

            def z1_transposes(r):
                pe.wait_ge(z1_ok, r.count(1, 1))
                if r.past():
                    pe.wait_ge(z1_lok, r.count(1, 0))
                if r.past(3):
                    pe.wait_ge(gelu_ok, r.count(HC, -HC))
                transposes(F[1], Z1).then_inc(z1_t, 1)

            def project(r, n):
                if n == 0:
                    pe.wait_ge(z1_hok, r.count(1, 1))
                    if r.past():
                        pe.wait_ge(masked, r.count(HALVES * TILES, -1))
                elif n == OUTS - 1:
                    pe.wait_ge(proj_out, r.count(OUTS, 1))
                w = slice(n * P, (n + 1) * P)
                high_passes(R[n % 3][:, :], wp_h[:, r.layer, w], wp_l[:, r.layer, w], z1_h[:, :])
                if n == 0:
                    pe.wait_ge(z1_lok, r.count(1, 1))
                low_pass(R[n % 3][:, :], wp_h[:, r.layer, w], z1_l[:, :]).then_inc(projected, 1)

            def play(s, has_r, has_f, fin, lst, tail):
                r, f = s.after(1), s
                st, ly, fly = r.stream, r.layer, f.layer

                def by_token():
                    pe.wait_ge(proj_out, r.count(OUTS, 2))
                    transposes(R[1], k_in).then_inc(tm_t, 1)
                    pe.wait_ge(proj_out, r.count(OUTS, 3))
                    transposes(R[2], v_in).then_inc(tm_t, 1)

                def z2_transposes():
                    pe.wait_ge(z2_ok, f.count(2, 1))
                    if f.past():
                        pe.wait_ge(res2, f.count(1, 0))
                    transposes(F2, Z2, range(PAIR))
                    pe.wait_ge(z2_ok, f.count(2, 2))
                    transposes(F2, Z2, range(PAIR, TILES)).then_inc(z2_t, 1)

                def ffn1(parts):
                    w = [slice(n * P, (n + 1) * P) for n in range(HC)]
                    for n in parts:
                        if n == 0:
                            pe.wait_ge(z2_hok, f.count(1, 1))
                            pe.wait_ge(z1_lok, f.count(1, 2) if has_r else f.count(1, 1))
                            if has_r:
                                pe.wait_ge(sum_out, f.count(1, 1))
                            if tail is not None:
                                pe.wait_ge(ys_ok, tail.group(1, 1))
                        if n >= 2:
                            pe.wait_ge(gelu_ok, f.count(HC, n - 1))
                        high_passes(F[n % 2][:, :], w1_h[:, fly, w[n]], w1_l[:, fly, w[n]], z2_h[:, :])
                    if 0 in parts:
                        pe.wait_ge(z2_lok, f.count(1, 1))
                    for n in parts:
                        low_pass(F[n % 2][:, :], w1_h[:, fly, w[n]], z2_l[:, :]).then_inc(ffn1_done, 1)

                def whole_sums():
                    if f.past():
                        pe.wait_ge(gelu_ok, f.count(HC, 0))
                    for t in range(TILES):
                        mm = nc.tensor.matmul(F[0][:, t * P:(t + 1) * P], kt[:, t, :], vt[:, t, :],
                                              start=True, stop=True, skip_group_check=True)
                    mm.then_inc(summed, 1)

                def half_sums():
                    pe.wait_ge(kt_ok, r.count(1, 1))
                    pe.wait_ge(vt_ok, r.count(1, 1))
                    if r.past():
                        pe.wait_ge(res1, r.count(2, 0))
                    for t in range(TILES):
                        mm = nc.tensor.matmul(M[:, t * P:(t + 1) * P], kt[0:HALF, t, :], vt[0:HALF, t, :],
                                              start=True, stop=True, skip_group_check=True)
                    mm.then_inc(half_summed, 1)

                def z4_transposes():
                    pe.wait_ge(z4_ok, tail.group(1, 1))
                    if not has_f:
                        pe.wait_ge(ys_ok, tail.group(1, 0))
                    transposes(F[1], Z4).then_inc(z4_tt, 1)

                def last_product():
                    pe.wait_ge(z4_tok, tail.group(1, 1))
                    for t in range(TILES):
                        mm = nc.tensor.matmul(F[1][:, t * P:(t + 1) * P], z4_t[:, t * P:(t + 1) * P], ws[:, :],
                                              start=True, stop=True, skip_group_check=True)
                    mm.then_inc(signed, 1)

                def scores(t, halves=range(HALVES)):
                    for h in halves:
                        n = HALVES * t + h
                        if n == 0:
                            pe.wait_ge(qx_ok, r.count(1, 1))
                            pe.wait_ge(kx_act, r.count(1, 1))
                            pe.wait_ge(kx_dve, r.count(1, 1))
                            pe.wait_ge(tanh_ok, r.count(1, 1))
                        elif n == 1:
                            pe.wait_ge(kt_ok, r.count(1, 1))
                        elif n > 2:
                            pe.wait_ge(masked, r.count(HALVES * TILES, n - 2))
                        for c in range(h * CHUNKS // HALVES, (h + 1) * CHUNKS // HALVES):
                            at, w = S_AT[c] - h * S_HALF, DEPTH[c]
                            mm = nc.tensor.matmul(
                                R[n % 3][:, at:at + QUAD * w].rearrange("p (g n) -> p g n", g=QUAD),
                                kx[:, t * CHUNKS + c, :, :], qx[:, :, t, c * CHUNK:c * CHUNK + w],
                                start=True, stop=True, skip_group_check=True)
                        mm.then_inc(scored, 1)

                def retention(t):
                    if t == 0:
                        if r.past():
                            pe.wait_ge(res1, r.count(2, 0))
                        if r.past(PHASES):
                            pe.wait_ge(state_ok, r.count(1, 1 - PHASES))
                        pe.wait_ge(vx_ok, r.count(1, 1))
                        pe.wait_ge(half_ok, r.count(1, 1))
                        pe.wait_ge(qd_ok, r.count(1, 1))
                    pe.wait_ge(masked, r.count(HALVES * TILES, HALVES * (t + 1)))
                    dst = M if t == TILES - 1 else RET
                    nc.tensor.matmul(dst[:, t * P:(t + 1) * P], state[:, ly, st, t, :], qd[:, t, :],
                                     start=True, stop=False, skip_group_check=True)
                    nc.tensor.matmul(dst[:, t * P + HALF:(t + 1) * P], half_state[:, t, :], qd[:, t, HALF:P],
                                     start=False, stop=False, skip_group_check=True)
                    for c in range(CHUNKS):
                        w = DEPTH[c]
                        for g in range(QUAD):
                            at = S_AT[c] + g * w
                            mm = nc.tensor.matmul(
                                dst[g * CHUNK:(g + 1) * CHUNK, t * P + c * CHUNK:t * P + c * CHUNK + w],
                                vx[:, t, c, g, :], S[t % 2][:, at:at + w],
                                start=False, stop=(c == CHUNKS - 1), skip_group_check=True)
                    mm.then_inc(ret_done, 1)

                def ffn2(t):
                    if t == 0:
                        pe.wait_ge(gelu_ok, f.count(HC, HC))
                        pe.wait_ge(z2_lok, f.count(1, 1))
                    for c in range(HC):
                        mm = nc.tensor.matmul(F2[:, t * P:(t + 1) * P], hid[:, c, t, :], w2[:, fly, c, :],
                                              start=(c == 0), stop=(c == HC - 1), skip_group_check=True)
                    if t == TILES - 1:
                        mm.then_inc(ffn2_done, 1)

                def output_projection():
                    for h, dst in enumerate((RET, M)):
                        pe.wait_ge(gated_ok, r.count(2, h + 1))
                        for t in range(h * PAIR, (h + 1) * PAIR):
                            mm = nc.tensor.matmul(dst[:, t * P:(t + 1) * P], gated[:, t, :], wo[:, ly, :],
                                                  start=True, stop=True, skip_group_check=True)
                        mm.then_inc(reto_done, 1)

                if has_r:
                    project(r, 1)
                    project(r, 2)
                if tail is not None:
                    z4_transposes()
                if has_r and has_f:
                    whole_sums()
                if has_r:
                    by_token()
                if tail is not None:
                    last_product()
                if has_r:
                    project(r, 3)
                if has_f:
                    z2_transposes()
                if has_r:
                    half_sums()
                if has_r and not has_f:
                    other_biases()
                if has_f:
                    ffn1([0, 1])
                if has_r:
                    scores(0, [0])
                if has_f:
                    ffn1([2])
                    ffn1([3])
                if has_r:
                    scores(0, [1])
                    scores(1, [0])
                if has_f:
                    for t in range(TILES):
                        ffn2(t)
                if has_r:
                    scores(1, [1])
                    retention(0)
                    scores(2)
                    retention(1)
                    scores(3, [0])
                    if not r.final:
                        z1_transposes(r.after(1))
                    scores(3, [1])
                    retention(2)
                    if not r.final:
                        project(r.after(1), 0)
                    retention(3)
                if has_r and not has_f:
                    pe.wait_ge(prep, PREP_ALL)
                    pe.wait_ge(prep_pool, PREP_POOL)
                if has_r:
                    output_projection()

            pe.wait_ge(first_params, FIRST_PARAMS_IN)
            for n in range(OUTS):
                mm = bias(n, wp[:, 0, n * P:(n + 1) * P], COL_B1)
            mm.then_inc(prep_pe, 1)
            z1_transposes(Turn(0, 0))
            pe.wait_ge(prep, PREP_W)
            project(Turn(0, 0), 0)
            run(pe, play)

        @block.scalar
        def _(act):
            def high_part(dst, src):
                return nc.scalar.activation(dst, src, ACT.Copy)

            def z1_high(r):
                act.wait_ge(z1_t, r.count(1, 1))
                if r.past():
                    act.wait_ge(projected, r.count(OUTS, 0))
                high_part(z1_h[:, :], F[1][:, :]).then_inc(z1_hok, 1)

            def by_tile(ap):
                return ap.rearrange("p (t n) -> p t n", t=TILES)

            def projection(r, n):
                act.wait_ge(projected, r.count(OUTS, n + 1))
                at = r.layer * OUTS + n
                src = by_tile(R[n % 3][:, :])
                nc.scalar.activation((q_in, k_in, v_in, xo_in)[n][:, :, :], src, IDENTITY,
                                     bias=pbias[:, at:at + 1]).then_inc(proj_out, 1)

            def queries(r, quadrants):
                if 0 in quadrants:
                    act.wait_ge(proj_out, r.count(OUTS, 1))
                    if r.past():
                        act.wait_ge(scored, r.count(HALVES * TILES, 0))
                for g in quadrants:
                    rows_g = slice(g * CHUNK, (g + 1) * CHUNK)
                    ins = nc.scalar.copy(qx[rows_g, g, :, :], q_in[rows_g, :, :])
                if g == QUAD - 1:
                    ins.then_inc(qx_ok, 1)

            def play(s, has_r, has_f, fin, lst, tail):
                r, f = s.after(1), s
                ly, fly = r.layer, f.layer

                def tanh():
                    nc.scalar.activation(th[:, :, :], by_tile(R[(OUTS - 1) % 3][:, :]), ACT.Tanh, scale=0.5,
                                         bias=hbias[:, ly:ly + 1]).then_inc(tanh_ok, 1)

                def keys(j):
                    if j == KX_DVE:
                        act.wait_ge(proj_out, r.count(OUTS, 2))
                    ins = nc.scalar.activation(kx[:, :, j, :], k_in[:, :, :].rearrange("p t (c n) -> p (t c) n", c=CHUNKS),
                                               ACT.Copy, scale=con[:, C_JM + j:C_JM + j + 1])
                    if j == QUAD - 1:
                        ins.then_inc(kx_act, 1)

                def values():
                    act.wait_ge(tm_t, r.count(2, 2))
                    nc.scalar.activation(vt[:, :, :], by_tile(R[2][:, :]), ACT.Copy).then_inc(vt_ok, 1)

                def spread_values(c):
                    if c == 0:
                        act.wait_ge(vt_ok, r.count(1, 1))
                        if r.past():
                            act.wait_ge(ret_done, r.count(TILES, 0))
                    v = vt[c * CHUNK:(c + 1) * CHUNK, :, :].rearrange("p t (g j e) -> p t g j e", g=QUAD, j=QUAD)
                    for j in range(QUAD):
                        ins = nc.scalar.copy(
                            vx[j * CHUNK:(j + 1) * CHUNK, :, c, :, j * DH:(j + 1) * DH], v[:, :, :, j, :])
                    if c == CHUNKS - 1:
                        ins.then_inc(vx_ok, 1)

                def z2_high():
                    act.wait_ge(z2_t, f.count(1, 1))
                    if f.past():
                        act.wait_ge(ffn1_done, f.count(HC, 0))
                    high_part(z2_h[:, :], F2[:, :]).then_inc(z2_hok, 1)

                def gelu(n):
                    act.wait_ge(ffn1_done, f.count(HC, n + 1))
                    if n == 0 and f.past():
                        act.wait_ge(ffn2_done, f.count(1, 0))
                    nc.scalar.activation(hid[:, n, :, :], by_tile(F[n % 2][:, :]), ACT.Gelu,
                                         bias=f1bias[:, fly * HC + n:fly * HC + n + 1]).then_inc(gelu_ok, 1)

                def last_transposed():
                    act.wait_ge(z4_tt, tail.group(1, 1))
                    nc.scalar.activation(z4_t[:, :], F[1][:, :], ACT.Copy).then_inc(z4_tok, 1)

                if has_r:
                    projection(r, 1)
                    projection(r, 2)
                    queries(r, [QUAD - 1])
                if tail is not None:
                    last_transposed()
                if has_r:
                    values()
                    projection(r, 3)
                if has_f:
                    z2_high()
                if has_r:
                    tanh()
                    for j in range(KX_DVE, QUAD):
                        keys(j)
                if has_f:
                    for n in range(HC):
                        gelu(n)
                if has_r and not has_f:
                    act.wait_ge(prep, PREP_ALL)
                if has_r:
                    for c in range(CHUNKS):
                        spread_values(c)
                    if not r.final:
                        z1_high(r.after(1))
                        projection(r.after(1), 0)
                        queries(r.after(1), range(QUAD - 1))

            act.dma_start(wp[:, :, :], proj_w.rearrange("l p n -> p l n")).then_inc(first_params, 16)
            act.dma_start(col[:, :], columns).then_inc(first_params, 16)
            act.dma_start(w1[:, :, :], ffn1_w.rearrange("l p n -> p l n")).then_inc(params, 16)
            act.dma_start(w2[:, :, :, :], ffn2_w.rearrange("l (c p) n -> p l c n", p=P)).then_inc(params, 16)
            z1_high(Turn(0, 0))
            act.wait_ge(prep, PREP_B)
            projection(Turn(0, 0), 0)
            act.wait_ge(zeroed, 1)
            queries(Turn(0, 0), range(QUAD - 1))
            act.wait_ge(zeroed, 2)
            run(act, play)

        @block.vector
        def _(dve):
            def sums(src, st, h):
                for t in range(h * PAIR, (h + 1) * PAIR):
                    ins = nc.vector.bn_stats(st[:, t, :], src[:, t, :])
                return ins

            def mean_and_variance(mv, st, h):
                nc.vector.memset(idle[:, h:h + 1], 0.0)
                for t in range(h * PAIR, (h + 1) * PAIR):
                    ins = nc.vector.bn_aggr(mv[:, t, :], st[:, t, :])
                return ins

            def statistics(src, st, mv, chain, value):
                for h in range(TILES // PAIR):
                    sums(src, st, h).then_inc(chain, 1)
                for h in range(TILES // PAIR):
                    dve.wait_ge(chain, value(h + 1))
                    last = mean_and_variance(mv, st, h)
                last.then_inc(chain, 1)
                dve.wait_ge(chain, value(3))

            def normalise(dst, src, mv, rs, tiles=range(TILES)):
                for t in tiles:
                    ins = nc.vector.tensor_scalar(dst[:, t, :], src[:, t, :], mv[:, t, 0:1], rs[:, t:t + 1],
                                                  ALU.subtract, ALU.mult)
                return ins

            def shifted(dst, mv):
                return nc.vector.tensor_scalar(dst, mv[:, :, 1], EPS, None, ALU.add)

            def first_norm(r):
                st = r.stream
                if r.layer == 0:
                    dve.wait_ge(x_in[st], r.step(16, 16))
                    statistics(xin[st], st1, mv1, ln1, lambda k: r.count(4, k))
                    shifted(vv1[:, X0_PART, :], mv1)
                    nc.vector.tensor_scalar(vv1[:, 0, :], mv1[:, :, 1], 1.0 + EPS, EPS * EPS,
                                            ALU.mult, ALU.add).then_inc(ln1, 1)
                else:
                    dve.wait_ge(res2, r.count(1, -1))
                    statistics(X[st], st1, mv1, ln1, lambda k: r.count(4, k))
                    shifted(vv1[:, 0, :], mv1).then_inc(ln1, 1)

            def first_normalise(r):
                dve.wait_ge(rs1_ok, r.count(1, 1))
                if r.past():
                    dve.wait_ge(z1_t, r.count(1, 0))
                src = X[r.stream] if r.layer else xin[r.stream]
                normalise(Z1, src, mv1, rs1[:, 0, :]).then_inc(z1_ok, 1)

            def input_normalise(r):
                if r.layer == 0:
                    dve.wait_ge(rs0_ok, r.group(1, 1))
                    normalise(X[r.stream], xin[r.stream], mv1, rs1[:, X0_PART, :]).then_inc(x0_ok, 1)

            def low_part(r, dst, src, high, sem_h, sem_l):
                dve.wait_ge(sem_h, r.count(1, 1))
                nc.vector.tensor_tensor(dst[:, :], src[:, :], high[:, :].bitcast(F32), ALU.subtract).then_inc(sem_l, 1)

            def by_tile(ap):
                return ap.rearrange("p (t n) -> p t n", t=TILES)

            def other_biases():
                dve.wait_ge(prep_pe, 2)
                nc.vector.tensor_tensor(pbias[:, OUTS:], F[0][:, OUTS:LAYERS * OUTS], col[:, COL_PB + OUTS:COL_F1B],
                                        ALU.add).then_inc(prep, 1)
                nc.vector.tensor_tensor(f1bias[:, :], F[0][:, LAYERS * OUTS:LAYERS * (OUTS + HC)],
                                        col[:, COL_F1B:COL_F1B + LAYERS * HC], ALU.add).then_inc(prep, 1)
                dve.wait_ge(prep, PREP_ALL - 1)
                nc.vector.tensor_scalar(hbias[:, 1:2], pbias[:, 2 * OUTS - 1:2 * OUTS], 0.5, None,
                                        ALU.mult).then_inc(prep, 1)

            def play(s, has_r, has_f, fin, lst, tail):
                r, f = s.after(1), s
                fst = f.stream

                def add_retention(h):
                    dve.wait_ge(reto_done, f.count(2, h + 1))
                    pair = slice(h * PAIR, (h + 1) * PAIR)
                    nc.vector.tensor_tensor(X[fst][:, pair, :], by_tile((RET, M)[h][:, :])[:, pair, :],
                                            X[fst][:, pair, :], ALU.add).then_inc(res1, 1)

                def second_norm():
                    dve.wait_ge(xb1, f.count(1, 1))
                    add_retention(0)
                    dve.wait_ge(res1, f.count(2, 1))
                    sums(X[fst], st2, 0).then_inc(ln2, 1)
                    add_retention(1)
                    dve.wait_ge(ln2, f.count(6, 1))
                    mean_and_variance(mv2, st2, 0).then_inc(ln2, 1)
                    dve.wait_ge(res1, f.count(2, 2))
                    sums(X[fst], st2, 1).then_inc(ln2, 1)
                    dve.wait_ge(ln2, f.count(6, 2))
                    shifted(vv2[:, 0:PAIR], mv2[:, 0:PAIR, :]).then_inc(ln2, 1)
                    dve.wait_ge(ln2, f.count(6, 3))
                    mean_and_variance(mv2, st2, 1).then_inc(ln2, 1)
                    dve.wait_ge(ln2, f.count(6, 5))
                    shifted(vv2[:, PAIR:], mv2[:, PAIR:, :]).then_inc(ln2, 1)

                def second_normalise():
                    if f.past():
                        dve.wait_ge(z2_t, f.count(1, 0))
                    for h in range(TILES // PAIR):
                        dve.wait_ge(rs2_ok, f.count(2, h + 1))
                        normalise(Z2, X[fst], mv2, rs2, range(h * PAIR, (h + 1) * PAIR)).then_inc(z2_ok, 1)

                def add_feed_forward():
                    dve.wait_ge(ffn2_done, f.count(1, 1))
                    dve.wait_ge(xb2, f.count(1, 1))
                    dst = XO if f.layer == LAYERS - 1 else X
                    nc.vector.tensor_tensor(dst[fst][:, :, :], by_tile(F2[:, :]), X[fst][:, :, :],
                                            ALU.add).then_inc(res2, 1)

                def decayed_queries():
                    dve.wait_ge(proj_out, r.count(OUTS, 1))
                    if r.past():
                        dve.wait_ge(ret_done, r.count(TILES, 0))
                    nc.vector.tensor_tensor(qd[:, :, :], q_in[:, :, :], over_tiles(con[:, C_DQ:C_DQ + P]),
                                            ALU.mult).then_inc(qd_ok, 1)

                def keys_by_token():
                    dve.wait_ge(tm_t, r.count(2, 1))
                    if r.past():
                        dve.wait_ge(summed, r.count(1, 0))
                    nc.vector.tensor_tensor(kt[:, :, :], by_tile(R[1][:, :]), over_tiles(con[:, C_DK:C_DK + P]),
                                            ALU.mult).then_inc(kt_ok, 1)

                def keys(j):
                    if j == 0:
                        dve.wait_ge(proj_out, r.count(OUTS, 2))
                        if r.past():
                            dve.wait_ge(scored, r.count(HALVES * TILES, 0))
                    k = k_in[:, :, :].rearrange("p t (c n) -> p (t c) n", c=CHUNKS)
                    ins = nc.vector.tensor_scalar(kx[:, :, j, :], k, con[:, C_JM + j:C_JM + j + 1], None, ALU.mult)
                    if j == KX_DVE - 1:
                        ins.then_inc(kx_dve, 1)

                def gates():
                    dve.wait_ge(tanh_ok, r.count(1, 1))
                    if r.past():
                        dve.wait_ge(gated_ok, r.count(2, 0))
                    nc.vector.scalar_tensor_tensor(out=gate[:, :, :], in0=th[:, :, :], scalar=1.0, in1=xo_in[:, :, :],
                                                   op0=ALU.add, op1=ALU.mult).then_inc(gate_ok, 1)

                def half_sums():
                    dve.wait_ge(half_summed, r.count(1, 1))
                    if r.past():
                        dve.wait_ge(ret_done, r.count(TILES, 0))
                    nc.vector.tensor_tensor(half_state[:, :, :], by_tile(M[:, :]), over_tiles(con[:, C_BM:C_BM + P]),
                                            ALU.mult).then_inc(half_ok, 1)

                def whole_sums():
                    dve.wait_ge(summed, f.count(1, 1))
                    if f.past():
                        dve.wait_ge(state_ok, f.count(1, 0))
                    nc.vector.tensor_tensor(state_sum[:, :, :], by_tile(F[0][:, :]), state[:, f.layer, fst, :, :],
                                            ALU.add).then_inc(sum_out, 1)

                def mask(t, halves=range(HALVES)):
                    if 0 in halves and (t >= 2 or r.past()):
                        dve.wait_ge(ret_done, r.count(TILES, t - 1))
                    for h in halves:
                        n = HALVES * t + h
                        dve.wait_ge(scored, r.count(HALVES * TILES, n + 1))
                        nc.vector.tensor_tensor(S[t % 2][:, h * S_HALF:(h + 1) * S_HALF], R[n % 3][:, 0:S_HALF],
                                                con[:, C_CM:C_CM + S_HALF], ALU.mult).then_inc(masked, 1)

                def apply_gates():
                    dve.wait_ge(gate_ok, r.count(1, 1))
                    if r.past():
                        dve.wait_ge(reto_done, r.count(2, 0))
                    first, last = slice(0, TILES - 1), slice(TILES - 1, TILES)
                    dve.wait_ge(ret_done, r.count(TILES, TILES - 1))
                    nc.vector.tensor_tensor(gated[:, first, :], by_tile(RET[:, :])[:, first, :], gate[:, first, :],
                                            ALU.mult).then_inc(gated_ok, 1)
                    dve.wait_ge(ret_done, r.count(TILES, TILES))
                    nc.vector.tensor_tensor(gated[:, last, :], by_tile(M[:, :])[:, last, :], gate[:, last, :],
                                            ALU.mult).then_inc(gated_ok, 1)

                def final_norm():
                    dve.wait_ge(res2, fin.count(1, 1))
                    statistics(XO[fin.stream], st3, mv3, ln3, lambda k: fin.group(4, k))
                    shifted(vv3[:, :], mv3).then_inc(ln3, 1)

                def final_normalise():
                    dve.wait_ge(rs3_ok, fin.group(1, 1))
                    if fin.past_groups():
                        dve.wait_ge(yg_ok, fin.group(1, 0))
                    normalise(Y3, XO[fin.stream], mv3, rs3).then_inc(y3_ok, 1)

                def last_norm():
                    dve.wait_ge(u3_ok, lst.group(1, 1))
                    statistics(U3[lst.stream], st4, mv4, ln4, lambda k: lst.group(4, k))
                    shifted(vv4[:, :], mv4).then_inc(ln4, 1)

                def last_normalise():
                    dve.wait_ge(rs4_ok, lst.group(1, 1))
                    normalise(Z4, U3[lst.stream], mv4, rs4).then_inc(z4_ok, 1)

                def scale_last():
                    dve.wait_ge(signed, tail.group(1, 1))
                    nc.vector.tensor_tensor(YS[:, :, :], by_tile(F[1][:, :]), over_tiles(row[:, ROW_SC, :]),
                                            ALU.mult).then_inc(ys_ok, 1)

                def add_row(dst, a, n, op=ALU.add):
                    return nc.vector.tensor_tensor(dst[:, :, :], a[:, :, :], over_tiles(row[:, n, :]), op)

                def residual_input():
                    dve.wait_ge(y3_ok, fin.group(1, 1))
                    add_row(YG, Y3, ROW_LG, ALU.mult).then_inc(yg_ok, 1)
                    dve.wait_ge(yg_ok, fin.group(1, 1))
                    dve.wait_ge(xrb_ok, fin.group(1, 1))
                    nc.vector.tensor_tensor(U3[fin.stream][:, :, :], YG[:, :, :], XRB[fin.stream][:, :, :],
                                            ALU.add).then_inc(u3_ok, 1)

                def output():
                    dve.wait_ge(ys_ok, tail.group(1, 1))
                    add_row(YB, YS, ROW_BI).then_inc(yb_ok, 1)
                    dve.wait_ge(yb_ok, tail.group(1, 1))
                    nc.vector.tensor_scalar(YC[:, :, :], YB[:, :, :], CLIP, -CLIP, ALU.min, ALU.max).then_inc(yc_ok, 1)
                    dve.wait_ge(yc_ok, tail.group(1, 1))
                    dve.wait_ge(stored[tail.stream], tail.step(16, 16))
                    nc.vector.tensor_tensor(OUT[tail.stream][:, :, :], YC[:, :, :], U3[tail.stream][:, :, :],
                                            ALU.add).then_inc(out_ok, 1)

                if not has_f:
                    if fin is not None:
                        final_norm()
                    if lst is not None:
                        last_norm()
                    if fin is not None:
                        final_normalise()
                    if tail is not None:
                        scale_last()
                    if lst is not None:
                        last_normalise()
                    if fin is not None:
                        residual_input()
                    if tail is not None:
                        output()
                    if not has_r:
                        return
                if has_f:
                    second_norm()
                if has_r:
                    keys(0)
                if has_f:
                    second_normalise()
                if has_r:
                    keys_by_token()
                if tail is not None:
                    scale_last()
                if has_r and has_f:
                    whole_sums()
                if has_r:
                    keys(1)
                if has_f:
                    low_part(f, z2_l, F2, z2_h, z2_hok, z2_lok)
                if has_r:
                    keys(2)
                    half_sums()
                    decayed_queries()
                    gates()
                if has_r and not has_f:
                    other_biases()
                if has_r:
                    input_normalise(r)
                if fin is not None:
                    final_norm()
                if lst is not None:
                    last_norm()
                if has_r:
                    mask(0)
                    mask(1, [0])
                if fin is not None:
                    final_normalise()
                if has_f:
                    add_feed_forward()
                if has_r:
                    if not r.final:
                        first_norm(r.after(1))
                    mask(1, [1])
                    mask(2)
                    if not r.final:
                        first_normalise(r.after(1))
                    mask(3)
                    if not r.final:
                        dve.wait_ge(projected, r.count(OUTS, OUTS))
                        low_part(r.after(1), z1_l, F[1], z1_h, z1_hok, z1_lok)
                    apply_gates()
                if lst is not None:
                    last_normalise()

            first_norm(Turn(0, 0))
            first_normalise(Turn(0, 0))

            def split_weights(w, gain, w_g, w_h, w_l, before):
                nc.vector.tensor_scalar(w_g[:, 0, :], w[:, 0, :], col[:, gain:gain + 1], None,
                                        ALU.mult).then_inc(prep_dve, 1)
                dve.wait_ge(prep_dve, before + 1)
                nc.vector.tensor_copy(w_h[:, 0, :], w_g[:, 0, :]).then_inc(prep_dve, 1)
                dve.wait_ge(prep_dve, before + 2)
                nc.vector.tensor_tensor(w_l[:, 0, :], w_g[:, 0, :], w_h[:, 0, :].bitcast(F32),
                                        ALU.subtract).then_inc(prep, 1)

            dve.wait_ge(first_params, FIRST_PARAMS_IN)
            split_weights(wp, COL_G1, wp_g, wp_h, wp_l, 0)
            dve.wait_ge(prep_pe, 1)
            nc.vector.tensor_tensor(pbias[:, 0:OUTS], F[0][:, 0:OUTS], col[:, COL_PB:COL_PB + OUTS],
                                    ALU.add).then_inc(prep, 1)
            dve.wait_ge(prep, 2)
            nc.vector.tensor_scalar(hbias[:, 0:1], pbias[:, OUTS - 1:OUTS], 0.5, None, ALU.mult).then_inc(prep, 1)
            low_part(Turn(0, 0), z1_l, F[1], z1_h, z1_hok, z1_lok)
            dve.wait_ge(params, PARAMS_IN)
            nc.vector.tensor_scalar(wo[:, :, :], wo_in[:, :, :], 0.5, None, ALU.mult).then_inc(prep, 1)
            nc.vector.tensor_scalar(ws_ge[:, :], ws_in[:, :], 0.0, 2.0, ALU.is_ge, ALU.mult).then_inc(prep, 1)
            dve.wait_ge(prep, 5)
            nc.vector.tensor_scalar(ws[:, :], ws_ge[:, :], -1.0, None, ALU.add).then_inc(prep, 1)
            split_weights(w1, COL_G2, w1_g, w1_h, w1_l, 2)
            dve.wait_ge(zeroed, 2)
            run(dve, play)

        @block.gpsimd
        def _(pool):
            def add_row(dst, a, n, op=ALU.add):
                return nc.gpsimd.tensor_tensor(dst[:, :, :], a[:, :, :], over_tiles(row[:, n, :]), op)

            def inverse_root(dst, src, ready, value, done):
                pool.wait_ge(ready, value)
                nc.gpsimd.tensor_tensor(dst, src, power[:, 0:dst.shape[1]], ALU.pow).then_inc(done, 1)

            def carry_wait():
                nc.gpsimd.tensor_tensor(held[:, :], power[:, 0:1], power[:, 0:1], ALU.mult)

            def input_copy(r):
                st = r.stream
                pool.wait_ge(x_in[st], r.step(16, 16))
                if r.past_groups(STREAMS):
                    pool.wait_ge(u3_ok, r.group(1, -1))
                add_row(XRB[st], xin[st], ROW_LB).then_inc(xrb_ok, 1)

            def first_root(r):
                inverse_root(rs1[:, 0, :], vv1[:, 0, :], ln1, r.count(4, 4), rs1_ok)
                if r.layer == 0:
                    inverse_root(rs1[:, X0_PART, :], vv1[:, X0_PART, :], ln1, r.count(4, 4), rs0_ok)

            def first_bias(r):
                if r.layer == 0:
                    pool.wait_ge(x0_ok, r.group(1, 1))
                else:
                    pool.wait_ge(z1_ok, r.count(1, 1))
                add_row(X[r.stream], X[r.stream], ROW_RB + r.layer).then_inc(xb1, 1)

            def play(s, has_r, has_f, fin, lst, tail):
                r, f = s.after(1), s

                def residual_input():
                    pool.wait_ge(y3_ok, fin.group(1, 1))
                    add_row(YG, Y3, ROW_LG, ALU.mult).then_inc(yg_ok, 1)
                    pool.wait_ge(yg_ok, fin.group(1, 1))
                    pool.wait_ge(xrb_ok, fin.group(1, 1))
                    nc.gpsimd.tensor_tensor(U3[fin.stream][:, :, :], YG[:, :, :], XRB[fin.stream][:, :, :],
                                            ALU.add).then_inc(u3_ok, 1)

                def output():
                    pool.wait_ge(ys_ok, tail.group(1, 1))
                    add_row(YB, YS, ROW_BI).then_inc(yb_ok, 1)
                    pool.wait_ge(yb_ok, tail.group(1, 1))
                    carry_wait()
                    nc.gpsimd.tensor_scalar(YC[:, :, :], YB[:, :, :], CLIP, -CLIP, ALU.min, ALU.max).then_inc(yc_ok, 1)
                    pool.wait_ge(yc_ok, tail.group(1, 1))
                    pool.wait_ge(stored[tail.stream], tail.step(16, 16))
                    nc.gpsimd.tensor_tensor(OUT[tail.stream][:, :, :], YC[:, :, :], U3[tail.stream][:, :, :],
                                            ALU.add).then_inc(out_ok, 1)

                if has_f:
                    for h in range(TILES // PAIR):
                        pair = slice(h * PAIR, (h + 1) * PAIR)
                        inverse_root(rs2[:, pair], vv2[:, pair], ln2, f.count(6, 4 + 2 * h), rs2_ok)
                    pool.wait_ge(z2_ok, f.count(2, 2))
                    add_row(X[f.stream], X[f.stream], ROW_F2B + f.layer).then_inc(xb2, 1)
                if has_r and has_f:
                    pool.wait_ge(sum_out, f.count(1, 1))
                    nc.gpsimd.tensor_tensor(state[:, f.layer, f.stream, :, :], state_sum[:, :, :],
                                            over_tiles(con[:, C_SM:C_SM + P]), ALU.mult).then_inc(state_ok, 1)
                if tail is not None and has_f:
                    output()
                if fin is not None:
                    inverse_root(rs3[:, :], vv3[:, :], ln3, fin.group(4, 4), rs3_ok)
                if fin is not None and has_f:
                    residual_input()
                if lst is not None:
                    inverse_root(rs4[:, :], vv4[:, :], ln4, lst.group(4, 4), rs4_ok)
                if has_r and not r.final:
                    first_root(r.after(1))
                if fin is not None and not fin.last_time:
                    input_copy(fin.after(2))
                if has_r:
                    first_bias(r)

            nc.gpsimd.memset(power[:, :], -0.5)
            nc.gpsimd.memset(qx[:, :, :, :], 0.0).then_inc(zeroed, 1)
            pool.wait_ge(zeroed, 1)
            first_root(Turn(0, 0))
            nc.gpsimd.memset(state[:, :, :, :, :], 0.0)
            nc.gpsimd.memset(vx[:, :, :, :, :], 0.0).then_inc(zeroed, 1)
            for s in range(STREAMS):
                nc.gpsimd.memset(OUT[s][:, :, :], 0.0).then_inc(stored[s], 16)
            pool.wait_ge(params, PARAMS_IN)
            for n, (w, gain, w_g, w_h, w_l) in enumerate(((wp, COL_G1, wp_g, wp_h, wp_l), (w1, COL_G2, w1_g, w1_h, w1_l))):
                nc.gpsimd.tensor_scalar(w_g[:, 1, :], w[:, 1, :], col[:, gain + 1:gain + 2], None,
                                        ALU.mult).then_inc(prep_pool, 1)
                pool.wait_ge(prep_pool, 3 * n + 1)
                nc.gpsimd.tensor_copy(w_h[:, 1, :], w_g[:, 1, :]).then_inc(prep_pool, 1)
                pool.wait_ge(prep_pool, 3 * n + 2)
                nc.gpsimd.tensor_tensor(w_l[:, 1, :], w_g[:, 1, :], w_h[:, 1, :].bitcast(F32),
                                        ALU.subtract).then_inc(prep_pool, 1)
            for st in range(STREAMS):
                input_copy(Turn(0, st))
            run(pool, play)


def constants():
    head = np.arange(P) // DH
    gamma = 1.0 - 2.0 ** (-5.0 - head.astype(np.float64))
    n = np.arange(P)
    con = np.zeros((P, CONSTS), np.float64)
    con[:, C_DQ:C_DQ + P] = gamma[:, None] ** n[None, :]
    con[:, C_DK:C_DK + P] = gamma[None, :] ** -n[:, None].astype(np.float64)
    con[:, C_BM:C_BM + P] = head[:, None] == head[None, :]
    con[:, C_SM:C_SM + P] = con[:, C_BM:C_BM + P] * gamma[:, None] ** P
    con[:, C_ID:C_ID + P] = np.eye(P)
    j, m = n // CHUNK, n % CHUNK
    decay = []
    for c in range(CHUNKS // HALVES):
        lag = np.arange(DEPTH[c])[None, :] - m[:, None]
        for g in range(QUAD):
            decay.append((lag >= 0) * gamma[(QUAD * g + j) * DH][:, None] ** np.maximum(lag, 0))
    con[:, C_CM:C_CM + S_HALF] = np.concatenate(decay, axis=1)
    con[:, C_JM:C_JM + QUAD] = (head[:, None] % QUAD) == np.arange(QUAD)[None, :]
    return con.astype(np.float32)


def kernel(**inputs):
    import concourse.bacc as bacc
    from concourse.bass_utils import run_bass_kernel_spmd

    a = {n: np.ascontiguousarray(v) for n, v in inputs.items()}

    def by_partition(v):
        return v.reshape(-1, P).T

    columns = np.concatenate([by_partition(a["L0_attn_" + n]) for n in (
        "ln1_g", "ln1_b", "ln2_g", "ln2_b", "proj_b", "ffn1_b")], axis=1)
    rows = np.concatenate([a[n].reshape(-1, WIDTH) for n in (
        "L0_attn_reto_b", "L0_attn_ffn2_b", "L0_attn_lnf_g", "L0_attn_lnf_b", "L0_ffn_scale", "L0_ffn_bias")], axis=0)
    arrays = {
        "x": a["L0_attn_x"], "columns": columns, "rows": rows, "consts": constants(),
        "proj_w": a["L0_attn_proj_w"], "reto_w": a["L0_attn_reto_w"], "ffn1_w": a["L0_attn_ffn1_w"],
        "ffn2_w": a["L0_attn_ffn2_w"], "sign_w": a["L0_ffn_weights"].T,
    }
    arrays = {n: np.ascontiguousarray(v) for n, v in arrays.items()}
    nc = bacc.Bacc("TRN2", target_bir_lowering=False, num_devices=1)
    args = [nc.dram_tensor(n + "_dram", v.shape, mybir.dt.from_np(v.dtype), kind="ExternalInput").ap()
            for n, v in arrays.items()]
    out = nc.dram_tensor("out_dram", arrays["x"].shape, F32, kind="ExternalOutput").ap()
    retention_ffn(nc, *args, out)
    r = run_bass_kernel_spmd(nc, [{n + "_dram": v for n, v in arrays.items()}], core_ids=[0])
    return r.results[0]["out_dram"]
```
